# Optimizing a Trainium2 kernel written in Bass

```python
import numpy as np
import jax
import jax.numpy as jnp

def _softmax(x, axis=-1):
    return jax.nn.softmax(x, axis=axis)

def _gelu(x):
    return jax.nn.gelu(x, approximate=True)

def _silu(x):
    return jax.nn.silu(x)

def _sigmoid(x):
    return jax.nn.sigmoid(x)

def _layernorm(x, axis=-1, eps=1e-05):
    m = jnp.mean(x, axis=axis, keepdims=True)
    v = jnp.var(x, axis=axis, keepdims=True)
    return (x - m) / jnp.sqrt(v + eps)

def _scatter_add(tgt, idx, src, axis=0):
    return tgt.at[idx].add(src)

def _segment_sum(src, seg, n):
    return jax.ops.segment_sum(src, seg, n)
kernel_name = 'mk_gnn_ffn_d1_gnn_r8_de1eea'

def setup_inputs(seed: int=0):
    np.random.seed(seed)
    _w = jnp.asarray

    def _rec_inputs():
        import jax
        import jax.numpy as jnp
        _gk = jax.random.key(seed)
        x = -8.776e-05 + 1 * jax.random.normal(jax.random.fold_in(_gk, 1), (1250, 512), jnp.float32)
        src = jax.random.randint(jax.random.fold_in(_gk, 2), (20000,), 0, 1250, jnp.int32)
        dst = jax.random.randint(jax.random.fold_in(_gk, 3), (20000,), 0, 1250, jnp.int32)
        _o = jnp.argsort(dst, stable=True)
        src = src[_o]
        dst = dst[_o]
        return (x, src, dst)
    x, src, dst = _rec_inputs()

    def _L0_gnn_setup():
        import jax, jax.numpy as jnp
        import numpy as np
        N_NODES = 1250
        N_EDGES = 20000
        IN_DIM = 512
        HID = 256
        HEADS = 4
        OUT_DIM = 512
        NEG_SLOPE = 0.2

        def _glorot(key, shape):
            fan_in, fan_out = (shape[0], shape[-1])
            lim = jnp.sqrt(6.0 / (fan_in + fan_out))
            return jax.random.uniform(key, shape, jnp.float32, -lim, lim)

        def gat_conv(x, src, dst, W, att_src, att_dst, bias):
            N = x.shape[0]
            h = (x @ W).reshape(N, HEADS, HID)
            a_src = jnp.sum(h * att_src, axis=-1)
            a_dst = jnp.sum(h * att_dst, axis=-1)
            e = jax.nn.leaky_relu(a_src[src] + a_dst[dst], NEG_SLOPE)
            m = jax.ops.segment_max(e, dst, num_segments=N)
            e = jnp.exp(e - m[dst])
            s = jax.ops.segment_sum(e, dst, num_segments=N)
            alpha = e / (s[dst] + 1e-16)
            msg = alpha[:, :, None] * h[src]
            out = jax.ops.segment_sum(msg, dst, num_segments=N)
            return out.reshape(N, HEADS * HID) + bias
        key = jax.random.key(seed)
        ks = jax.random.split(key, 16)
        x = jax.random.normal(ks[0], (N_NODES, IN_DIM), jnp.float32)
        edge_index = jax.random.randint(ks[1], (2, N_EDGES), 0, N_NODES, jnp.int64)
        W1 = _glorot(ks[2], (IN_DIM, HEADS * HID))
        att_src1 = _glorot(ks[3], (HEADS, HID))
        att_dst1 = _glorot(ks[4], (HEADS, HID))
        b1 = jnp.zeros((HEADS * HID,), jnp.float32)
        W2 = _glorot(ks[5], (HEADS * HID, HEADS * HID))
        att_src2 = _glorot(ks[6], (HEADS, HID))
        att_dst2 = _glorot(ks[7], (HEADS, HID))
        b2 = jnp.zeros((HEADS * HID,), jnp.float32)
        fcW = _glorot(ks[8], (HEADS * HID, OUT_DIM))
        fcb = jnp.zeros((OUT_DIM,), jnp.float32)
        return dict(x=x, edge_index=edge_index, W1=W1, att_src1=att_src1, att_dst1=att_dst1, b1=b1, W2=W2, att_src2=att_src2, att_dst2=att_dst2, b2=b2, fcW=fcW, fcb=fcb)
    _L0_gnn_all = _L0_gnn_setup()
    _L0_gnn_in = {k: v for k, v in _L0_gnn_all.items() if k in ('W1', 'att_src1', 'att_dst1', 'b1', 'W2', 'att_src2', 'att_dst2', 'b2', 'fcW', 'fcb')}
    del _L0_gnn_all

    def _L0_ffn_setup():
        import jax, jax.numpy as jnp
        import numpy as np
        DIM = 512
        NE = 8
        TOPK = 2
        CF = 1.2
        HID = 4 * DIM
        B, S = (8, 512)
        key = jax.random.key(seed)
        ks = jax.random.split(key, 4)
        s = 0.02
        return {'x': jax.random.normal(ks[0], (B, S, DIM), jnp.float32), 'gate_w': jax.random.normal(ks[1], (NE, DIM), jnp.float32) * s, 'gate_b': jnp.zeros((NE,), jnp.float32), 'w1': jax.random.normal(ks[2], (NE, DIM, HID), jnp.float32) * s, 'b1': jnp.zeros((NE, HID), jnp.float32), 'w2': jax.random.normal(ks[3], (NE, HID, DIM), jnp.float32) * s, 'b2': jnp.zeros((NE, DIM), jnp.float32)}
    _L0_ffn_all = _L0_ffn_setup()
    _L0_ffn_in = {k: v for k, v in _L0_ffn_all.items() if k in ('gate_w', 'gate_b', 'w1', 'b1', 'w2', 'b2')}
    del _L0_ffn_all
    return {'x': x, 'src': src, 'dst': dst, 'L0_gnn_W1': _L0_gnn_in['W1'], 'L0_gnn_att_src1': _L0_gnn_in['att_src1'], 'L0_gnn_att_dst1': _L0_gnn_in['att_dst1'], 'L0_gnn_b1': _L0_gnn_in['b1'], 'L0_gnn_W2': _L0_gnn_in['W2'], 'L0_gnn_att_src2': _L0_gnn_in['att_src2'], 'L0_gnn_att_dst2': _L0_gnn_in['att_dst2'], 'L0_gnn_b2': _L0_gnn_in['b2'], 'L0_gnn_fcW': _L0_gnn_in['fcW'], 'L0_gnn_fcb': _L0_gnn_in['fcb'], 'L0_ffn_gate_w': _L0_ffn_in['gate_w'], 'L0_ffn_gate_b': _L0_ffn_in['gate_b'], 'L0_ffn_w1': _L0_ffn_in['w1'], 'L0_ffn_b1': _L0_ffn_in['b1'], 'L0_ffn_w2': _L0_ffn_in['w2'], 'L0_ffn_b2': _L0_ffn_in['b2']}

def reference(x, src, dst, L0_gnn_W1, L0_gnn_att_src1, L0_gnn_att_dst1, L0_gnn_b1, L0_gnn_W2, L0_gnn_att_src2, L0_gnn_att_dst2, L0_gnn_b2, L0_gnn_fcW, L0_gnn_fcb, L0_ffn_gate_w, L0_ffn_gate_b, L0_ffn_w1, L0_ffn_b1, L0_ffn_w2, L0_ffn_b2):
    import jax
    import jax.numpy as jnp

    def _L0_gnn_ref(x, edge_index, W1, att_src1, att_dst1, b1, W2, att_src2, att_dst2, b2, fcW, fcb):
        import jax, jax.numpy as jnp
        import numpy as np
        N_NODES = 1250
        N_EDGES = 20000
        IN_DIM = 512
        HID = 256
        HEADS = 4
        OUT_DIM = 512
        NEG_SLOPE = 0.2

        def _glorot(key, shape):
            fan_in, fan_out = (shape[0], shape[-1])
            lim = jnp.sqrt(6.0 / (fan_in + fan_out))
            return jax.random.uniform(key, shape, jnp.float32, -lim, lim)

        def gat_conv(x, src, dst, W, att_src, att_dst, bias):
            N = x.shape[0]
            h = (x @ W).reshape(N, HEADS, HID)
            a_src = jnp.sum(h * att_src, axis=-1)
            a_dst = jnp.sum(h * att_dst, axis=-1)
            e = jax.nn.leaky_relu(a_src[src] + a_dst[dst], NEG_SLOPE)
            m = jax.ops.segment_max(e, dst, num_segments=N)
            e = jnp.exp(e - m[dst])
            s = jax.ops.segment_sum(e, dst, num_segments=N)
            alpha = e / (s[dst] + 1e-16)
            msg = alpha[:, :, None] * h[src]
            out = jax.ops.segment_sum(msg, dst, num_segments=N)
            return out.reshape(N, HEADS * HID) + bias
        N = x.shape[0]
        loops = jnp.arange(N, dtype=edge_index.dtype)
        src = jnp.concatenate([edge_index[0], loops])
        dst = jnp.concatenate([edge_index[1], loops])
        h = gat_conv(x, src, dst, W1, att_src1, att_dst1, b1)
        h = jax.nn.relu(h)
        h = gat_conv(h, src, dst, W2, att_src2, att_dst2, b2)
        h = jax.nn.relu(h)
        return h @ fcW + fcb

    def _L0_ffn_ref(x, gate_w, gate_b, w1, b1, w2, b2):
        import jax, jax.numpy as jnp
        import numpy as np
        DIM = 512
        NE = 8
        TOPK = 2
        CF = 1.2
        HID = 4 * DIM
        B, S = (8, 512)
        Bq, Sq, D = x.shape
        T = Bq * Sq
        cap = int(CF * T / NE)
        xf = x.reshape(T, D)
        probs = jax.nn.softmax(xf @ gate_w.T + gate_b, axis=-1)
        topw, topi = jax.lax.top_k(probs, TOPK)
        onehot = jax.nn.one_hot(topi, NE, dtype=topw.dtype)
        w_te = jnp.einsum('tk,tke->te', topw, onehot)
        routed = onehot.sum(axis=1) > 0
        wm = jnp.where(routed, w_te, -1.0)
        sel_w, sel_idx = jax.lax.top_k(wm.T, cap)
        sel_w = jnp.maximum(sel_w, 0.0)
        xg = xf[sel_idx]
        h = jax.nn.gelu(jnp.einsum('ecd,edh->ech', xg, w1) + b1[:, None, :], approximate=False)
        out = jnp.einsum('ech,ehd->ecd', h, w2) + b2[:, None, :]
        weighted = out * sel_w[..., None]
        of = jnp.zeros((T, D), x.dtype).at[sel_idx.reshape(-1)].add(weighted.reshape(-1, D))
        return of.reshape(Bq, Sq, D)
    edge_index = jnp.stack([src, dst])
    x = x + _L0_gnn_ref(_layernorm(x, axis=-1), edge_index, L0_gnn_W1, L0_gnn_att_src1, L0_gnn_att_dst1, L0_gnn_b1, L0_gnn_W2, L0_gnn_att_src2, L0_gnn_att_dst2, L0_gnn_b2, L0_gnn_fcW, L0_gnn_fcb)
    x = x + _L0_ffn_ref(_layernorm(x, axis=-1)[None], L0_ffn_gate_w, L0_ffn_gate_b, L0_ffn_w1, L0_ffn_b1, L0_ffn_w2, L0_ffn_b2)[0]
    return x

_drawn_inputs = setup_inputs


def setup_inputs(seed=0):
    import zlib

    import numpy as np

    out = dict(_drawn_inputs(seed))
    spreads = {'L0_gnn_b1': (0.0, 0.1),
     'L0_gnn_b2': (0.0, 0.1),
     'L0_gnn_fcb': (0.0, 0.1),
     'L0_ffn_gate_b': (0.0, 0.416),
     'L0_ffn_b1': (0.0, 0.594),
     'L0_ffn_b2': (0.0, 0.314)}
    factors = {'L0_gnn_att_dst1': 6.123, 'L0_gnn_att_src2': 7.296, 'L0_gnn_att_dst2': 23.282}
    for name, (base, spread) in spreads.items():
        noise = np.random.default_rng([zlib.crc32(name.encode()), seed]).standard_normal(out[name].shape)
        drawn = base * np.exp(spread * noise) if base else spread * noise
        out[name] = jnp.asarray(drawn.astype(out[name].dtype))
    for name, factor in factors.items():
        out[name] = (out[name] * factor).astype(out[name].dtype)
    return out
```

```python
import numpy as np
from contextlib import ExitStack

import concourse.bass as bass
from concourse import mybir
from concourse.bass import ds

N, E = 1250, 20000
D, HEADS, HID, C1 = 512, 4, 256, 1024
NE, TOPK, FF = 8, 2, 2048
CAP = int(1.2 * N / NE)
SLOPE, EPS_LN, EPS_SM = 0.2, 1e-5, 1e-16

P = 125
NT = N // P
HALF = 5 * P
HX = HID + 1
CE = 125
NCH = E // CE
CR = NCH // 2
GC = 4
NG = NCH // GC
CAPP = 188
TS = CAPP // 2
SLOTS = NE * CAPP
NO_SLOT = SLOTS
FM = FF // 128
KD = D // 128
KC = C1 // 128
MASKED = -1e30
RING = 5
SIDES = 8 * HEADS + 2


def program(nc, x, src, dst, W1, as1, ad1, b1, W2, as2, ad2, b2, fcW, fcb,
            gate_w, gate_b, w1, mb1, w2, mb2, out):
    dt, ALU, ACT, AX = mybir.dt, mybir.AluOpType, mybir.ActivationFunctionType, mybir.AxisListType
    f32, bf16, f16, i32, i16 = dt.float32, dt.bfloat16, dt.float16, dt.int32, dt.int16

    xg = nc.dram_tensor("xg", [SLOTS, D], f32, kind="Internal").ap()
    eo = nc.dram_tensor("eo", [SLOTS + 1, D], f32, kind="Internal").ap()

    with ExitStack() as ctx:
        def sb(name, shape, d=f32):
            return ctx.enter_context(nc.sbuf_tensor(name, shape, d))

        def sem(name):
            return ctx.enter_context(nc.semaphore(name))

        areaA = sb("areaA", [128, NT * HEADS * HX])
        areaB = sb("areaB", [128, KC * N])
        areaC = sb("areaC", [128, NT * N])
        areaW = sb("areaW", [128, KC * C1])

        def view(area, at, n, d=f32):
            size = {f32: 1, i32: 1}.get(d, 2)
            cols = -(-n // size)
            v = area[:, at:at + cols]
            return (v if d == f32 else v.bitcast(d))[:, 0:n], at + cols

        a = 0
        wideI, a = view(areaA, a, 2 * N - P, bf16)
        iotaN, a = view(areaA, a, N, f16)
        edgeT, a = view(areaA, a, 2 * NCH)
        ohS, a = view(areaA, a, GC * N, bf16)
        ohD, a = view(areaA, a, GC * 126, bf16)
        ctmp, a = view(areaA, a, 2 * N)
        edgeI, a = view(areaA, a, 4 * CE, i32)
        edgeF, a = view(areaA, a, 4 * CE)
        grpI, a = view(areaA, a, GC * CE, i32)
        grpF, a = view(areaA, a, GC * CE)
        assert a <= NT * HEADS * HX
        ohS = ohS.rearrange("p (g n) -> p g n", g=GC)
        ohD = ohD.rearrange("p (g n) -> p g n", g=GC)
        ctmp = ctmp.rearrange("p (g n) -> p g n", g=2)
        edgeI = edgeI.rearrange("p (g n) -> p g n", g=4)
        edgeF = edgeF.rearrange("p (g n) -> p g n", g=4)
        hx = areaA[:, :].rearrange("p (t h c) -> p t h c", t=NT, h=HEADS)
        W1s = areaB[:, 0:KD * C1].rearrange("p (k c) -> p k c", k=KD)
        xnT = areaB[:, KD * C1:KD * C1 + KD * N].rearrange("p (k n) -> p k n", k=KD)
        featT = areaB[:, :].rearrange("p (k n) -> p k n", k=KC)
        CT, _ = view(areaC, 0, NT * N, i16)
        mask, _ = view(areaC, NT * N // 2, NT * N, bf16)
        CT = CT.rearrange("p (t n) -> p t n", t=NT)
        mask = mask.rearrange("p (t n) -> p t n", t=NT)
        a = 0
        xn2, a = view(areaC, a, NT * D)
        xn2 = xn2.rearrange("p (t d) -> p t d", t=NT)
        xn2T, a = view(areaC, a, 2 * KD * P)
        xn2T = xn2T.rearrange("p (b k n) -> p b k n", b=2, k=KD)
        fcb_bc, a = view(areaC, a, D)
        cmp1, a = view(areaC, a, NT * NE * NE)
        cmp2, a = view(areaC, a, NT * NE * NE)
        wmT, a = view(areaC, a, N)
        ohT, a = view(areaC, a, 2 * N)
        prob, a = view(areaC, a, NT * NE)
        wm, a = view(areaC, a, NT * NE)
        rank8, a = view(areaC, a, NT * NE)
        oh2, a = view(areaC, a, 2 * NT * NE)
        cnt, a = view(areaC, a, 3 * 2 * NT)
        prob, wm, rank8 = [v.rearrange("p (t e) -> p t e", t=NT) for v in (prob, wm, rank8)]
        oh2 = oh2.rearrange("p (k t e) -> p k t e", k=2, t=NT)
        cnt = cnt.rearrange("p (a k t) -> p a k t", a=3, k=2)
        assert a <= NT * N
        cmp1 = cmp1.rearrange("p (t a b) -> p t a b", t=NT, a=NE)
        cmp2 = cmp2.rearrange("p (t a b) -> p t a b", t=NT, a=NE)
        ohT = ohT.rearrange("p (k n) -> p k n", k=2)
        xs = areaW[:, 0:NT * D].rearrange("p (t d) -> p t d", t=NT)
        W2s = areaW[:, :].rearrange("p (k c) -> p k c", k=KC)
        fcWs = areaW[:, 0:KC * D].rearrange("p (k c) -> p k c", k=KC)
        junk = areaW[:, KC * D:KC * D + 2 * N].rearrange("p (b n) -> p b n", b=2)
        junk2 = areaW[:, KC * D + 2 * N:KC * D + 2 * N + 2 * P].rearrange("p (b n) -> p b n", b=2)
        WSZ = KD * FF
        w1s = [v[:, 0:WSZ].rearrange("p (k c) -> p k c", k=KD) for v in (areaA, areaB)]
        w2s = [v[:, 0:WSZ].rearrange("p (k c) -> p k c", k=FM) for v in (areaC, areaW)]
        hT = areaC[:, WSZ:WSZ + FM * CAPP].rearrange("p (m n) -> p m n", m=FM)
        xring = areaA[:, WSZ:WSZ + 2 * D].rearrange("p (b d) -> p b d", b=2)
        xgT = areaB[:, WSZ:WSZ + 2 * KD * CAPP].rearrange("p (b k n) -> p b k n", b=2, k=KD)

        work = sb("work", [128, NT * D + 2 * 2 * D])
        att_bc = work[:, 0:2 * C1].rearrange("p (a c) -> p a c", a=2)
        watt = work[:, 2 * C1:4 * C1].rearrange("p (a c) -> p a c", a=2)
        ring = work[:, 0:(4 + RING) * HALF].rearrange("p (r n) -> p r n", r=4 + RING)
        rbc = [[ring[:, 0], ring[:, 1]], [ring[:, 2], ring[:, 3]]]
        pring = ring[:, 4:4 + RING]
        osum = work[:, (4 + RING) * HALF:(4 + RING) * HALF + 5 * HX].rearrange("p (t c) -> p t c", t=5)
        junkb = work[:, (4 + RING) * HALF:(4 + RING) * HALF + N].bitcast(bf16).rearrange("p (b n) -> p b n", b=2)
        x2 = work[:, 0:NT * D].rearrange("p (t d) -> p t d", t=NT)

        identF = sb("identF", [128, 128])
        identB = sb("identB", [128, 128], bf16)
        byhead = sb("byhead", [8, 9 * P + N + 2 * P])
        sel = byhead[0:8, 0:9 * P].rearrange("p (r n) -> p r n", r=9)
        rowsA = byhead[0:8, 9 * P:9 * P + N]
        rowsR = rowsA
        selcur = byhead[0:8, 9 * P + N:].rearrange("p (r n) -> p r n", r=2)
        xr = areaA[:, WSZ:WSZ + 2 * 2 * D].rearrange("p (b t d) -> p b t d", b=2, t=2)
        er = work[:, NT * D:NT * D + 2 * 2 * D].rearrange("p (b t d) -> p b t d", b=2, t=2)
        yT = areaC[:, WSZ + FM * CAPP:WSZ + FM * CAPP + 2 * CAPP].rearrange("p (b n) -> p b n", b=2)
        grow = areaW[:, 0:8 * D].rearrange("p (b d) -> p b d", b=8)
        small = sb("small", [128, 1620])
        s = 0

        def sm(n, d=f32):
            nonlocal s
            v, s = view(small, s, n, d)
            return v
        wa = [sm(KD * 8).rearrange("p (k r) -> p k r", k=KD), sm(KC * 8).rearrange("p (k r) -> p k r", k=KC)]
        asd = sm(NT * 8).rearrange("p (t r) -> p t r", t=NT)
        as02 = sm(NT * 4).rearrange("p (t r) -> p t r", t=NT)
        mx = sm(NT * 4).rearrange("p (t r) -> p t r", t=NT)
        mlk = sm(NT * 4).rearrange("p (t r) -> p t r", t=NT)
        rr = sm(NT * 8).rearrange("p (t r) -> p t r", t=NT)
        stat = sm(NT * 6).rearrange("p (t r) -> p t r", t=NT)
        mv = sm(NT * 2).rearrange("p (t r) -> p t r", t=NT)
        sd = sm(NT)
        rstd = sm(NT)
        rsum = sm(10).rearrange("p (t r) -> p t r", t=2)
        b1cols = sm(128)
        vcols = sm(48)
        gwT = sm(KD * NE).rearrange("p (k e) -> p k e", k=KD)
        gb_bc = sm(NE)
        ones = sm(128)
        gmm = sm(2)
        gdiag = sm(2 * NG).rearrange("p (a g) -> p a g", a=2)
        tlo = sm(1)
        thi = sm(1)
        gup = sm(NG)
        gdn = sm(NG)
        hit = sm(NG)
        hit2 = sm(NG)
        hitv = sm(2 * NG).rearrange("p (a g) -> p a g", a=2)
        bnd = sm(4)
        tri10 = sm(NT)
        bndI = sm(3 * NT, i32)
        red = sm(NT)
        red2 = sm(NT)
        eiota = sm(NE)
        lowE = sm(NE * NE).rearrange("p (a b) -> p a b", a=NE)
        lowP = sm(P)
        g2 = sm(2 * NT).rearrange("p (k t) -> p k t", k=2)
        e2 = sm(2 * NT).rearrange("p (k t) -> p k t", k=2)
        keep = sm(2 * NT).rearrange("p (k t) -> p k t", k=2)
        slotI = sm(2 * NT, i32).rearrange("p (k t) -> p k t", k=2)
        assert s <= 1620, s
        vrow = areaA[:, 9400:9400 + 128]
        vrow2 = areaA[:, 9528:9528 + 128]
        vrow3 = areaA[:, 9656:9656 + D]
        zrow = areaC[:, 0:12 * D].rearrange("p (t d) -> p t d", t=12)

        PS = ctx.enter_context(nc.psum_tensor("PS", [128, 8 * 512], f32))

        def bank(b, n=512, p=128, at=0):
            return PS[0:p, 512 * b + at:512 * b + at + n]

        (l_edge, l_grp, l_x, l_W1, l_att0, l_att1, l_W2, l_fcW, l_v1, l_v2, l_v3, l_fcb, l_gb, l_zero,
         l_outs) = [sem("l_" + n) for n in
                    "edge grp x W1 att0 att1 W2 fcW v1 v2 v3 fcb gb zero outs".split()]
        l_xr = [sem("l_x0"), sem("l_x1")]
        (pool_const, edge_f, grp_f, edge_T, edge_cols, g_bc, g_cols, g_rows, g_ready, v_T, v_cols) = [
            sem(n) for n in ("pool_const edge_f grp_f edge_T edge_cols g_bc g_cols g_rows g_ready v_T v_cols").split()]
        var_eps, std, xn_ready, xn_T, xnT_ready = [sem(n) for n in "var_eps std xn_ready xn_T xnT_ready".split()]
        oh_ready, oh_free, c_done, ctmp_ready, mask_ready, c_T, ct_ready = [
            sem(n) for n in "oh_ready oh_free c_done ctmp_ready mask_ready c_T ct_ready".split()]
        watt_ready, watt_used, wa_ready = [sem(n) for n in "watt_ready watt_used wa_ready".split()]
        rows_mm, rows_ready, cols_T, cols_ready, mbc, m_tile, h_mm, h_ready, r_cols, r_T, rowsR_ready = [
            sem(n) for n in
            "rows_mm rows_ready cols_T cols_ready mbc m_tile h_mm h_ready r_cols r_T rowsR_ready".split()]
        sel_cur, sel_used, side_mm, side_out, low_ready, top_ready, exp_ready, p_ready, p_used, sums, o_dve, \
            o_act, o_norm = [sem(n) for n in
                             "sel_cur sel_used side_mm side_out low_ready top_ready exp_ready p_ready p_used "
                             "sums o_dve o_act o_norm".split()]
        fc_mm, x2b, x2_ready, xr_used = [sem(n) for n in "fc_mm x2b x2_ready xr_used".split()]
        var2, std2, xn2_ready, xn2_T, xn2T_ready, lg_mm, lg_sub, lg_exp = [
            sem(n) for n in "var2 std2 xn2_ready xn2_T xn2T_ready lg_mm lg_sub lg_exp".split()]
        routed, rt_T, rt_rows, cnt_mm, cnt_used, slots_ready, scat = [
            sem(n) for n in "routed rt_T rt_rows cnt_mm cnt_used slots_ready scat".split()]
        w1_in = [sem("w1_in0"), sem("w1_in1")]
        w2_in = [sem("w2_in0"), sem("w2_in1")]
        xr_in = [sem("xr_in0"), sem("xr_in1")]
        xg_T, xgT_ready, up_mm, up_ready, dn_mm, y_ready, y_T, er_ready = [
            sem(n) for n in "xg_T xgT_ready up_mm up_ready dn_mm y_ready y_T er_ready".split()]
        er_out = [sem("er_out0"), sem("er_out1")]
        fetched = [sem(f"fetched{i}") for i in range(4)]
        sum_ready, s_eps, s_inv = sem("sum_ready"), sem("s_eps"), sem("s_inv")
        settled = sem("settled")
        zeros_ready = sem("zeros_ready")
        CONST = {n: i + 1 for i, n in enumerate("ones tlo thi gup gdn eiota iotaN tri10 identB wideI lowE lowP sel hx".split())}
        dve_step, act_step, pool_step = sem("dve_step"), sem("act_step"), sem("pool_step")

        class Steps:
            def __init__(self, eng, sm_):
                self.eng, self.sem, self.n = eng, sm_, 0

            def link(self, ins):
                ins.then_inc(self.sem, 1)
                self.n = self.n + 1
                self.eng.wait_ge(self.sem, self.n)

        block = ctx.enter_context(nc.Block())

        @block.sync
        def _(sp):
            sp.dma_start(edgeI[0:CR, 0:2, :], src.rearrange("(r p k) -> p r k", r=2, p=CR)).then_inc(l_edge, 16)
            sp.dma_start(edgeI[0:CR, 2:4, :], dst.rearrange("(r p k) -> p r k", r=2, p=CR)).then_inc(l_edge, 16)
            sp.dma_start(grpI[0:NG, :], dst.rearrange("(g k) -> g k", g=NG)).then_inc(l_grp, 16)
            sp.dma_start(xs[0:P, :, :], x.rearrange("(t p) d -> p t d", p=P)).then_inc(l_x, 16)
            sp.dma_start(W1s[:, :, :], W1.rearrange("(k p) c -> p k c", p=128)).then_inc(l_W1, 16)
            sp.dma_start(vrow, mb1.rearrange("e (m p) -> (e m) p", p=128)).then_inc(l_v1, 16)
            sp.dma_start(vrow2[0:32, :], mb2.rearrange("e (m p) -> (e m) p", p=128)).then_inc(l_v2, 16)
            sp.dma_start(vrow2[32:40, :], b1.rearrange("(m p) -> m p", p=128)).then_inc(l_v2, 16)
            sp.dma_start(vrow2[40:48, :], b2.rearrange("(m p) -> m p", p=128)).then_inc(l_v2, 16)
            sp.dma_start(vrow3[0:NE, :], gate_w).then_inc(l_v3, 16)
            sp.dma_start(gb_bc[0:P, :], gate_b.rearrange("(a e) -> a e", a=1).to_broadcast([P, NE])).then_inc(l_gb, 16)
            sp.wait_ge(zeros_ready, 1)
            sp.dma_start(xg[0:12 * 124, :].rearrange("(p t) d -> p t d", t=12), zrow[0:124, :, :]).then_inc(l_zero, 16)
            sp.dma_start(xg[12 * 124:SLOTS, :], zrow[0:SLOTS - 12 * 124, 0, :]).then_inc(l_zero, 16)
            sp.dma_start(eo[SLOTS:SLOTS + 1, :], zrow[0:1, 0, :]).then_inc(l_zero, 16)
            sp.wait_ge(xn_T, NT)
            sp.dma_start(W2s[:, :, :], W2.rearrange("(k p) c -> p k c", p=128)).then_inc(l_W2, 16)
            sp.wait_ge(h_mm, 2 * 2 * NT)
            sp.dma_start(fcWs[:, :, :], fcW.rearrange("(k p) c -> p k c", p=128)).then_inc(l_fcW, 16)
            sp.wait_ge(sums, 5 * 2 * 2 * HEADS)
            sp.dma_start(fcb_bc[0:P, :], fcb.rearrange("(a e) -> a e", a=1).to_broadcast([P, D])).then_inc(l_fcb, 16)
            for t in range(NT):
                if t >= 2:
                    sp.wait_ge(xr_used, t - 1)
                sp.dma_start(xring[0:P, t % 2, :], x[P * t:P * t + P, :]).then_inc(l_xr[t % 2], 16)

            w1_v = w1.rearrange("e (k p) c -> e p k c", p=128)
            w2_v = w2.rearrange("e (k p) c -> e p k c", p=128)
            sp.dma_start(w1s[0][:, :, :], w1_v[0]).then_inc(w1_in[0], 16)
            sp.wait_ge(fc_mm, NT)
            sp.dma_start(w1s[1][:, :, :], w1_v[1]).then_inc(w1_in[1], 16)
            sp.wait_ge(cnt_used, 2 * NT)
            sp.dma_start(w2s[1][:, :, :], w2_v[1]).then_inc(w2_in[1], 16)
            sp.wait_ge(scat, 16 * 2 * NT)
            sp.dma_start(w2s[0][:, :, :], w2_v[0]).then_inc(w2_in[0], 16)

            def load_rows(e, par):
                sp.dma_start(xr[0:TS, par, :, :],
                             xg[ds(e * CAPP, CAPP), :].rearrange("(t p) d -> p t d", p=TS)).then_inc(xr_in[par], 16)

            def store_rows(e, par):
                sp.wait_ge(er_ready, 4 * e + 4)
                sp.dma_start(eo[ds(e * CAPP, CAPP), :].rearrange("(t p) d -> p t d", p=TS),
                             er[0:TS, par, :, :]).then_inc(er_out[par], 16)
            load_rows(0, 0)
            load_rows(1, 1)
            with sp.Fori(0, NE // 2 - 1) as q:
                for par in range(2):
                    e = q * 2 + par
                    sp.wait_ge(xg_T, 2 * e + 2)
                    load_rows(e + 2, par)
                    sp.wait_ge(up_mm, FM * e + FM)
                    sp.dma_start(w1s[par][:, :, :], w1_v[ds(e + 2, 1)].rearrange("a p k c -> p (a k) c")).then_inc(w1_in[par], 16)
                    sp.wait_ge(dn_mm, 4 * e + 4)
                    sp.dma_start(w2s[par][:, :, :], w2_v[ds(e + 2, 1)].rearrange("a p k c -> p (a k) c")).then_inc(w2_in[par], 16)
                    store_rows(e, par)
            for e in (NE - 2, NE - 1):
                store_rows(e, e % 2)
            for t in range(NT):
                sp.wait_ge(sum_ready, t + 1)
                sp.dma_start(out[P * t:P * t + P, :], x2[0:P, t, :]).then_inc(l_outs, 16)
            sp.wait_ge(l_outs, 16 * NT)

        @block.gpsimd
        def _(pool):
            st = Steps(pool, pool_step)
            g = nc.gpsimd
            st.link(g.memset(identF[:], 0.0))
            st.link(g.affine_select(out=identF[:], in_=identF[:], compare_op=ALU.not_equal, fill=1.0, base=0,
                                    pattern=[[-1, 128]], channel_multiplier=1))
            g.memset(ones[:], 1.0).then_inc(pool_const, 1)
            g.iota(tlo[0:NT, :], pattern=[[0, 1]], base=0, channel_multiplier=P,
                   allow_small_or_imprecise_dtypes=True).then_inc(pool_const, 1)
            g.iota(thi[0:NT, :], pattern=[[0, 1]], base=P - 1, channel_multiplier=P,
                   allow_small_or_imprecise_dtypes=True).then_inc(pool_const, 1)
            g.iota(gup[0:NT, :], pattern=[[1, NG]], base=1, channel_multiplier=0,
                   allow_small_or_imprecise_dtypes=True).then_inc(pool_const, 1)
            g.iota(gdn[0:NT, :], pattern=[[-1, NG]], base=NG, channel_multiplier=0,
                   allow_small_or_imprecise_dtypes=True).then_inc(pool_const, 1)
            g.iota(eiota[:, :], pattern=[[1, NE]], base=0, channel_multiplier=0,
                   allow_small_or_imprecise_dtypes=True).then_inc(pool_const, 1)
            g.iota(iotaN[:, :], pattern=[[1, N]], base=0, channel_multiplier=0,
                   allow_small_or_imprecise_dtypes=True).then_inc(pool_const, 1)
            st.link(g.memset(tri10[0:NT, :], 1.0))
            g.affine_select(out=tri10[0:NT, :], in_=tri10[0:NT, :], compare_op=ALU.is_gt, fill=0.0, base=0,
                            pattern=[[1, NT]], channel_multiplier=-1).then_inc(pool_const, 1)
            g.tensor_copy(identB[:], identF[:]).then_inc(pool_const, 1)
            g.memset(zrow[:, :, :], 0.0).then_inc(zeros_ready, 1)
            st.link(g.memset(wideI[:, :], 0.0))
            g.affine_select(out=wideI[:, :], in_=wideI[:, :], compare_op=ALU.not_equal, fill=1.0, base=N - P,
                            pattern=[[-1, 2 * N - P]], channel_multiplier=1).then_inc(pool_const, 1)
            st.link(g.memset(lowE[:, :, :], 1.0))
            g.affine_select(out=lowE[:, :, :], in_=lowE[:, :, :], compare_op=ALU.is_gt, fill=0.0, base=0,
                            pattern=[[1, NE], [-1, NE]], channel_multiplier=0).then_inc(pool_const, 1)
            st.link(g.memset(lowP[:, :], 1.0))
            g.affine_select(out=lowP[:, :], in_=lowP[:, :], compare_op=ALU.is_gt, fill=0.0, base=0,
                            pattern=[[-1, P]], channel_multiplier=1).then_inc(pool_const, 1)
            st.link(g.memset(sel[:, :, :], 0.0))
            g.affine_select(out=sel[:, :, :], in_=sel[:, :, :], compare_op=ALU.not_equal, fill=1.0, base=0,
                            pattern=[[-1, 9], [0, P]], channel_multiplier=1).then_inc(pool_const, 1)

            for l in range(2):
                av = ((as1, ad1), (as2, ad2))[l]
                if l:
                    pool.wait_ge(c_T, 3 * NT)
                    pool.wait_ge(v_cols, 3)
                    pool.wait_ge(mask_ready, NT)
                    g.memset(hx[:, :, :, HID:HX], 1.0).then_inc(pool_const, 1)
                    pool.wait_ge(watt_used, 2 * KD)
                for i in range(2):
                    pool.dma_start(att_bc[:, i, :], av[i].rearrange("(a h) c -> a (h c)", a=1).to_broadcast([128, C1]))\
                        .then_inc((l_att0, l_att1)[l], 16)
                pool.wait_ge((l_att0, l_att1)[l], 32)
                pool.wait_ge((l_W1, l_W2)[l], 16)
                for k in range((KD, KC)[l]):
                    for i in range(2):
                        n = 2 * k + i + 2 * KD * l
                        if n >= 2:
                            pool.wait_ge(watt_used, n - 1)
                        g.tensor_tensor(out=watt[:, i, :], in0=(W1s, W2s)[l][:, k, :], in1=att_bc[:, i, :],
                                        op=ALU.mult).then_inc(watt_ready, 1)

            def select_heads(l):
                with pool.Fori(0, HEADS + 1) as h:
                    n = h + l * (HEADS + 1)
                    pool.wait_ge(sel_used, n + 1)
                    for i in range(2):
                        ins = g.tensor_copy(selcur[:, i, :], sel[:, ds(h + 4 * i, 1), :].rearrange("p a n -> p (a n)"))
                        ins.then_inc(sel_cur, 1)
            for l in range(2):
                select_heads(l)
            pool.wait_ge(l_fcb, 16)
            pool.wait_ge(side_mm, 2 * SIDES)
            for t in range(NT):
                pool.wait_ge(l_xr[t % 2], 16 * (t // 2 + 1))
                g.tensor_tensor(out=x2[0:P, t, :], in0=xring[0:P, t % 2, :], in1=fcb_bc[0:P, :],
                                op=ALU.add).then_inc(xr_used, 1)
            pool.wait_ge(l_zero, 48)
            pool.wait_ge(slots_ready, 1)
            for t in range(NT):
                for k in range(2):
                    g.indirect_dma_start(out=xg, out_offset=bass.IndirectOffsetOnAxis(ap=slotI[0:P, k, t:t + 1], axis=0),
                                         in_=xn2[0:P, t, :], in_offset=None,
                                         bounds_check=SLOTS - 1, oob_is_err=False).then_inc(scat, 16)
            pool.wait_ge(er_out[0], 16 * NE // 2)
            pool.wait_ge(er_out[1], 16 * NE // 2)
            for i in range(2 * NT):
                t, k = i // 2, i % 2
                if i >= 4:
                    pool.wait_ge(sum_ready, (i - 4) // 2 + 1)
                g.indirect_dma_start(out=grow[0:P, i % 4, :], out_offset=None, in_=eo,
                                     in_offset=bass.IndirectOffsetOnAxis(ap=slotI[0:P, k, t:t + 1], axis=0),
                                     bounds_check=SLOTS, oob_is_err=False).then_inc(fetched[i % 4], 16)

        @block.scalar
        def _(act):
            sc = nc.scalar

            def settle():
                act.sem_inc(settled, 1)
            act.wait_ge(var_eps, 1)
            sc.activation(sd[0:P, :], sd[0:P, :], ACT.Sqrt).then_inc(std, 1)
            for t in range(NT):
                act.wait_ge(xn_T, t + 1)
                sc.activation(xnT[:, :, P * t:P * t + P],
                              bank(6 + t % 2, KD * P).rearrange("p (k n) -> p k n", k=KD), ACT.Copy).then_inc(xnT_ready, 1)

            def counts_out(t, par, first):
                act.wait_ge(c_done, t + 1)
                if not first:
                    act.wait_ge(c_T, 3 * t - 3)
                    act.wait_ge(mask_ready, t - 1)
                sc.activation(ctmp[0:P, par, :], PS[0:P, 1536 * par:1536 * par + N], ACT.Copy).then_inc(ctmp_ready, 1)

            def counts_T_out(t, par):
                for q in range(3):
                    b = (4, 4, 2)[q]
                    act.wait_ge(c_T, 3 * t + q + 1)
                    sc.activation(CT[0:P, 4 * q:4 * q + b, ds(t * P, P)],
                                  bank(6 + q % 2, b * P, P).rearrange("p (b n) -> p b n", b=b),
                                  ACT.Copy).then_inc(ct_ready, 1)
            act.wait_ge(l_zero, 48)
            counts_out(0, 0, True)
            counts_out(1, 1, True)
            counts_T_out(0, 0)
            with act.Fori(1, NT // 2) as q:
                for par in range(2):
                    counts_out(q * 2 + par, par, False)
                    counts_T_out(q * 2 + par - 1, 1 - par)
            counts_T_out(NT - 1, 1)

            def layer(l):
                act.wait_ge(rows_mm, l + 1)
                sc.activation(rowsA, PS[0:8, 0:N], ACT.Copy).then_inc(rows_ready, 1)
                for t in range(NT):
                    for c in range(2):
                        n = 2 * NT * l + 2 * t + c
                        act.wait_ge(h_mm, n + 1)
                        if n == 0:
                            act.wait_ge(pool_const, CONST["hx"])
                        sc.activation(hx[0:P, t, 2 * c:2 * c + 2, 0:HID],
                                      bank(6 + c, 512, P).rearrange("p (h n) -> p h n", h=2), ACT.Copy).then_inc(h_ready, 1)
                act.wait_ge(r_T, l + 1)
                for q in range(3):
                    n = (500, 500, 250)[q]
                    sc.activation(rowsR[:, 500 * q:500 * q + n], bank(q, n, 8), ACT.Copy).then_inc(rowsR_ready, 1)
                bcol = vcols[:, 32 + 8 * l:40 + 8 * l]

                def side(n, kind, half, h):
                    act.wait_ge(side_mm, n + 1)
                    settle()
                    if kind < 2:
                        ins = sc.activation(rbc[half][kind][0:P, :], PS[0:P, 2560:2560 + HALF], ACT.Copy)
                    else:
                        src_ = PS[:, 2560:2560 + 640].rearrange("p (t n) -> p t n", t=5)[:, :, 0:P]
                        k = 2 * h + kind - 2
                        dst_ = featT[:, ds(k, 1), HALF * half:HALF * half + HALF].rearrange("p a (t n) -> p (a t) n", t=5)
                        ins = sc.activation(dst_, src_, ACT.Relu, bias=bcol[:, ds(k, 1)])
                    ins.then_inc(side_out, 1)

                s0 = SIDES * l

                def sums_out(b, u, first):
                    if not first:
                        act.wait_ge(side_mm, s0 + 4 * u)
                    for it in (1, 3):
                        act.wait_ge(sums, b * 5 - 4 + it)
                        sc.activation(osum[0:P, it, :], bank(it, HX, P), ACT.Copy).then_inc(o_act, 1)

                def half_body(h, half, first, second=False):
                    u = 2 * h + half
                    b = 2 * HEADS * l + u
                    act.wait_ge(side_out, s0 + (2 if first else 4 if second else 4 * u - 2))
                    for j in range(NT + 1):
                        if j < NT:
                            if j < RING - 1 and not (first and l == 0):
                                act.wait_ge(p_used, (b - 1) * (NT - 1) + j + NT - RING + 1)
                            elif j == RING - 1 and not (first and l == 0):
                                act.wait_ge(sums, b * 5)
                            elif j >= RING:
                                act.wait_ge(p_used, b * (NT - 1) + j - RING + 1)
                            settle()
                            sc.activation(pring[0:P, j % RING, :], rbc[half][1][0:P, :], ACT.Identity,
                                          bias=as02[0:P, j, ds(h, 1)]).then_inc(low_ready, 1)
                        if j >= 1:
                            act.wait_ge(top_ready, b * NT + j)
                            sc.activation(pring[0:P, (j - 1) % RING, :], pring[0:P, (j - 1) % RING, :],
                                          ACT.Exp).then_inc(exp_ready, 1)
                        if j == 2 and not first:
                            sums_out(b, u, second)
                        if j in (5, 7):
                            side(s0 + 4 * u + (j - 5) // 2 + (2 if first else 0), (j - 5) // 2, 1 - half, h)
                        if j in (9, 10) and not first:
                            side(s0 + 4 * u + j - 7, j - 7, 1 - half, h - 1 + half)
                if l == 0:
                    act.wait_ge(watt_used, 2 * (KD + KC))
                side(s0, 0, 0, 0)
                side(s0 + 1, 1, 0, 0)
                half_body(0, 0, True)
                half_body(0, 1, False, True)
                with act.Fori(1, HEADS) as h:
                    half_body(h, 0, False)
                    half_body(h, 1, False)
                sums_out(2 * HEADS * (l + 1), 2 * HEADS, False)
                side(s0 + 8 * HEADS, 2, 1, HEADS - 1)
                side(s0 + 8 * HEADS + 1, 3, 1, HEADS - 1)
            for l in range(2):
                layer(l)

            for t in range(NT):
                act.wait_ge(var2, t + 1)
                sc.activation(sd[0:P, t:t + 1], sd[0:P, t:t + 1], ACT.Sqrt).then_inc(std2, 1)
                if t >= 1:
                    tokens_T_out = t - 1
                    act.wait_ge(xn2_T, t)
                    sc.activation(xn2T[:, (t - 1) % 2, :, :],
                                  bank(2 + (t - 1) % 2, KD * P).rearrange("p (k n) -> p k n", k=KD),
                                  ACT.Copy).then_inc(xn2T_ready, 1)
            act.wait_ge(xn2_T, NT)
            sc.activation(xn2T[:, (NT - 1) % 2, :, :],
                          bank(2 + (NT - 1) % 2, KD * P).rearrange("p (k n) -> p k n", k=KD),
                          ACT.Copy).then_inc(xn2T_ready, 1)
            act.wait_ge(lg_sub, 1)
            sc.activation(prob[0:P, :, :], prob[0:P, :, :], ACT.Exp).then_inc(lg_exp, 1)
            act.wait_ge(rt_T, 1)
            for q in range(3):
                n = (500, 500, 250)[q]
                sc.activation(wmT[0:8, 500 * q:500 * q + n], bank(q, n, 8), ACT.Copy).then_inc(rt_rows, 1)
            for k in range(2):
                act.wait_ge(rt_T, 2 + k)
                for q in range(3):
                    n = (500, 500, 250)[q]
                    sc.activation(ohT[0:8, k, 500 * q:500 * q + n], bank(3 * (1 - k) + q, n, 8),
                                  ACT.Copy).then_inc(rt_rows, 1)

            def expert(e, par):
                for q in range(2):
                    act.wait_ge(xg_T, 2 * e + q + 1)
                    sc.activation(xgT[:, par, 2 * q:2 * q + 2, :],
                                  bank(q, 2 * CAPP).rearrange("p (k n) -> p k n", k=2), ACT.Copy).then_inc(xgT_ready, 1)
                for m in range(FM):
                    act.wait_ge(up_mm, e * FM + m + 1)
                    settle()
                    sc.activation(hT[:, m, :], bank(2 + m % 2, CAPP), ACT.Gelu,
                                  bias=b1cols[:, ds(e * FM + m, 1)]).then_inc(up_ready, 1)
            with act.Fori(0, NE // 2) as q:
                for par in range(2):
                    expert(q * 2 + par, par)

        @block.vector
        def _(dve):
            v = nc.vector
            st = Steps(dve, dve_step)
            dve.wait_ge(l_x, 16)
            for t in range(NT):
                ins = v.bn_stats(out=stat[0:P, t, :], in_=xs[0:P, t, :])
            st.link(ins)
            for t in range(NT):
                ins = v.bn_aggr(out=mv[0:P, t, :], in_=stat[0:P, t, :])
            st.link(ins)
            v.tensor_scalar(sd[0:P, :], mv[0:P, :, 1], EPS_LN, None, ALU.add).then_inc(var_eps, 1)
            dve.wait_ge(l_grp, 16)
            st.link(v.tensor_copy(grpF[0:NG, :], grpI[0:NG, :]))
            dve.wait_ge(l_edge, 32)
            v.tensor_copy(edgeF[0:CR, :, :], edgeI[0:CR, :, :]).then_inc(edge_f, 1)
            v.tensor_reduce(out=gmm[0:NG, 0:1], in_=grpF[0:NG, :], axis=AX.X, op=ALU.min)
            st.link(v.tensor_reduce(out=gmm[0:NG, 1:2], in_=grpF[0:NG, :], axis=AX.X, op=ALU.max))
            dve.wait_ge(pool_const, CONST["gdn"])
            v.tensor_scalar(gdiag[0:NG, 0, :], identF[0:NG, 0:NG], gmm[0:NG, 0:1], None, ALU.mult)
            v.tensor_scalar(gdiag[0:NG, 1, :], identF[0:NG, 0:NG], gmm[0:NG, 1:2], None, ALU.mult).then_inc(g_cols, 1)
            dve.wait_ge(std, 1)
            st.link(v.reciprocal(rstd[0:P, :], sd[0:P, :]))
            for t in range(NT):
                v.tensor_scalar(xs[0:P, t, :], xs[0:P, t, :], mv[0:P, t, 0:1], rstd[0:P, t:t + 1],
                                ALU.subtract, ALU.mult).then_inc(xn_ready, 1)
            dve.wait_ge(edge_T, 1)
            v.tensor_copy(edgeT[0:CE, :], bank(0, 2 * NCH, CE)).then_inc(edge_cols, 1)
            dve.wait_ge(g_bc, 1)
            v.tensor_scalar(hit[0:NT, :], bank(1, NG, NT), thi[0:NT, :], None, ALU.is_le)
            st.link(v.tensor_scalar(hit2[0:NT, :], bank(1, NG, NT, NG), tlo[0:NT, :], None, ALU.is_ge))
            st.link(v.tensor_tensor(out=hit[0:NT, :], in0=hit[0:NT, :], in1=hit2[0:NT, :], op=ALU.mult))
            v.tensor_tensor(out=hitv[0:NT, 0, :], in0=hit[0:NT, :], in1=gup[0:NT, :], op=ALU.mult)
            st.link(v.tensor_tensor(out=hitv[0:NT, 1, :], in0=hit[0:NT, :], in1=gdn[0:NT, :], op=ALU.mult))
            v.tensor_reduce(out=bnd[0:NT, 1:2], in_=hitv[0:NT, 0, :], axis=AX.X, op=ALU.max)
            st.link(v.tensor_reduce(out=bnd[0:NT, 0:1], in_=hitv[0:NT, 1, :], axis=AX.X, op=ALU.max))
            v.tensor_scalar(bnd[0:NT, 0:1], bnd[0:NT, 0:1], -1.0, float(NG), ALU.mult, ALU.add)
            st.link(v.tensor_scalar(bnd[0:NT, 1:2], bnd[0:NT, 1:2], 1.0, None, ALU.max))
            st.link(v.tensor_scalar(bnd[0:NT, 3:4], bnd[0:NT, 1:2], -1.0, None, ALU.add))
            st.link(v.tensor_tensor(out=bnd[0:NT, 0:1], in0=bnd[0:NT, 0:1], in1=bnd[0:NT, 3:4], op=ALU.min))
            v.tensor_tensor(out=bnd[0:NT, 3:4], in0=bnd[0:NT, 0:1], in1=bnd[0:NT, 1:2], op=ALU.subtract)
            v.tensor_tensor(out=bnd[0:NT, 2:3], in0=bnd[0:NT, 1:2], in1=bnd[0:NT, 0:1],
                            op=ALU.subtract).then_inc(g_rows, 1)
            dve.wait_ge(g_rows, 2)
            v.tensor_copy(bndI[0:1, 0:2 * NT], bank(1, 2 * NT, 1, 128))
            v.tensor_scalar(bndI[0:1, 2 * NT:3 * NT], bank(1, NT, 1, 128 + 2 * NT), float(NG * NT), None,
                            ALU.add).then_inc(g_ready, 1)
            dve.wait_ge(v_T, 3)
            v.tensor_copy(b1cols[:, :], bank(2, 128)).then_inc(v_cols, 1)
            v.tensor_copy(vcols[:, :], bank(2, 48, 128, 128)).then_inc(v_cols, 1)
            v.tensor_copy(gwT[:, :, :], bank(2, KD * NE, 128, 256).rearrange("p (k e) -> p k e", k=KD)).then_inc(v_cols, 1)

            dve.wait_ge(pool_const, CONST["iotaN"])
            dve.wait_ge(g_ready, 1)

            def onehots(t):
                lo = dve.value_load(bndI[0:1, ds(t, 1)], min_val=0, max_val=NG * NT)
                hi = dve.value_load(bndI[0:1, ds(t + NT, 1)], min_val=1, max_val=NG * NT)
                shift = dve.value_load(bndI[0:1, ds(t + 2 * NT, 1)], min_val=0, max_val=NG * NT + NG)
                with dve.Fori(lo, hi) as r:
                    g = nc.s_assert_within(r + shift - NG * NT, 0, NG - 1)
                    for k in range(GC):
                        n = r * GC + k
                        dve.wait_ge(oh_free, n + 1)
                        v.tensor_scalar(ohD[0:CE, k, 0:P], iotaN[0:CE, ds(t * P, P)],
                                        edgeT[0:CE, ds(g * GC + (NCH + k), 1)], None, ALU.is_equal)
                        v.tensor_scalar(ohS[0:CE, k, :], iotaN[0:CE, :],
                                        edgeT[0:CE, ds(g * GC + k, 1)], None, ALU.is_equal).then_inc(oh_ready, 1)

            def make_mask(t, par):
                dve.wait_ge(ctmp_ready, t + 1)
                v.tensor_scalar(mask[0:P, ds(t, 1), :].rearrange("p a n -> p (a n)"), ctmp[0:P, par, :], 0.0, MASKED,
                                ALU.is_equal, ALU.mult).then_inc(mask_ready, 1)
            def att_sums(l, k):
                for i in range(2):
                    dve.wait_ge(watt_ready, 2 * k + i + 1 + 2 * KD * l)
                    v.tensor_reduce(out=wa[l][:, ds(k, 1), 4 * i:4 * i + 4],
                                    in_=watt[:, i, :].rearrange("p (h c) -> p h c", h=HEADS).unsqueeze(1),
                                    axis=AX.X, op=ALU.add).then_inc(watt_used, 1)
            onehots(0)
            onehots(1)
            make_mask(0, 0)
            with dve.Fori(1, NT // 2) as q:
                for par in range(2):
                    onehots(q * 2 + par)
                    make_mask(q * 2 + par - 1, 1 - par)
                att_sums(0, q - 1)
            make_mask(NT - 1, 1)

            def layer(l):
                nonlocal_n0 = l * 2 * HEADS * NT
                dve.wait_ge(cols_T, l + 1)
                st.link(v.tensor_copy(asd[0:P, :, :], bank(6, 8 * NT, P).rearrange("p (t r) -> p t r", t=NT)))
                cols_ready_ = v.tensor_scalar(as02[0:P, :, :], asd[0:P, :, 0:4], SLOPE, None, ALU.mult)
                cols_ready_.then_inc(cols_ready, 1)
                for h in range(HEADS):
                    dve.wait_ge(mbc, HEADS * l + h + 1)
                    for t in range(NT):
                        n = (HEADS * l + h) * NT + t
                        if n >= 2:
                            dve.wait_ge(m_tile, n - 1)
                        ins = v.tensor_tensor_reduce(out=junkb[0:P, t % 2, :], in0=mask[0:P, t, :],
                                                     in1=PS[0:P, 1536 * (h % 2):1536 * (h % 2) + N],
                                                     scale=1.0, scalar=MASKED * 10, op0=ALU.add, op1=ALU.max,
                                                     accum_out=mx[0:P, t, h:h + 1])
                        ins.then_inc(m_tile, 1)
                dve.wait_ge(m_tile, HEADS * NT * (l + 1))
                ad = asd[0:P, :, 4:8]
                st.link(v.tensor_tensor(out=mx[0:P, :, :], in0=mx[0:P, :, :], in1=ad, op=ALU.add))
                st.link(v.tensor_scalar(mlk[0:P, :, :], mx[0:P, :, :], SLOPE, None, ALU.mult))
                st.link(v.tensor_tensor(out=mx[0:P, :, :], in0=mx[0:P, :, :], in1=mlk[0:P, :, :], op=ALU.max))
                v.tensor_scalar(mlk[0:P, :, :], ad, SLOPE, None, ALU.mult)
                st.link(v.tensor_tensor(out=rr[0:P, :, 0:4], in0=ad, in1=mx[0:P, :, :], op=ALU.subtract))
                v.tensor_tensor(out=rr[0:P, :, 4:8], in0=mlk[0:P, :, :], in1=mx[0:P, :, :],
                                op=ALU.subtract).then_inc(r_cols, 1)
                if l == 0:
                    for k in range(KC):
                        att_sums(1, k)
                s0 = SIDES * l

                def weights(b, j, half):
                    dve.wait_ge(exp_ready, b * NT + j + 1)
                    p = pring[0:P, j % RING, :]
                    v.tensor_tensor(out=p, in0=p, in1=CT[0:P, j, HALF * half:HALF * half + HALF],
                                    op=ALU.mult).then_inc(p_ready, 1)

                def sums_out(b, u, first):
                    if not first:
                        dve.wait_ge(side_mm, s0 + 4 * u)
                    for it in (0, 2, 4):
                        dve.wait_ge(sums, b * 5 - 4 + it)
                        v.tensor_copy(osum[0:P, it, :], bank(it, HX, P)).then_inc(o_dve, 1)

                def divide(b):
                    dve.wait_ge(o_dve, 3 * b)
                    dve.wait_ge(o_act, 2 * b)
                    v.tensor_scalar(rsum[0:P, 0, :], osum[0:P, :, HID], EPS_SM, None, ALU.add).then_inc(s_eps, 1)
                    dve.wait_ge(s_eps, b)
                    v.reciprocal(rsum[0:P, 1, :], rsum[0:P, 0, :]).then_inc(s_inv, 1)
                    dve.wait_ge(s_inv, b)
                    v.tensor_tensor(out=osum[0:P, :, 0:HID], in0=osum[0:P, :, 0:HID],
                                    in1=rsum[0:P, 1, :].unsqueeze(2).to_broadcast([P, 5, HID]), op=ALU.mult).then_inc(o_norm, 1)

                def half_body(h, half, first, second=False):
                    u = 2 * h + half
                    b = 2 * HEADS * l + u
                    dve.wait_ge(side_out, s0 + (2 if first else 4 if second else 4 * u - 2))
                    for j in range(NT + 1):
                        if j < NT:
                            dve.wait_ge(low_ready, b * NT + j + 1)
                            p = pring[0:P, j % RING, :]
                            v.scalar_tensor_tensor(out=p, in0=rbc[half][0][0:P, :], scalar=asd[0:P, j, ds(h, 1)], in1=p,
                                                   op0=ALU.add, op1=ALU.max).then_inc(top_ready, 1)
                        if j >= 1:
                            weights(b, j - 1, half)
                        if j == 2 and not first:
                            sums_out(b, u, second)
                        if j == 4 and not first:
                            divide(b)
                half_body(0, 0, True)
                half_body(0, 1, False, True)
                with dve.Fori(1, HEADS) as h:
                    half_body(h, 0, False)
                    half_body(h, 1, False)
                sums_out(2 * HEADS * (l + 1), 2 * HEADS, False)
                divide(2 * HEADS * (l + 1))
            assert NT // 2 - 1 == KD
            for l in range(2):
                layer(l)

            for t in range(NT):
                dve.wait_ge(fc_mm, t + 1)
                dve.wait_ge(xr_used, t + 1)
                st.link(v.tensor_tensor(out=x2[0:P, t, :], in0=bank(t % 2, D, P), in1=x2[0:P, t, :], op=ALU.add))
                st.link(v.bn_stats(out=stat[0:P, t, :], in_=x2[0:P, t, :]))
                st.link(v.bn_aggr(out=mv[0:P, t, :], in_=stat[0:P, t, :]))
                v.tensor_scalar(sd[0:P, t:t + 1], mv[0:P, t, 1:2], EPS_LN, None, ALU.add).then_inc(var2, 1)
                dve.wait_ge(std2, t + 1)
                st.link(v.reciprocal(rstd[0:P, t:t + 1], sd[0:P, t:t + 1]))
                v.tensor_scalar(xn2[0:P, t, :], x2[0:P, t, :], mv[0:P, t, 0:1], rstd[0:P, t:t + 1],
                                ALU.subtract, ALU.mult).then_inc(xn2_ready, 1)
            dve.wait_ge(lg_mm, NT)
            dve.wait_ge(l_gb, 16)
            pr = prob[0:P, :, :]

            def over_tiles(col):
                return col.unsqueeze(1).to_broadcast([P, NT, NE])

            def over_experts(col):
                return col.unsqueeze(2).to_broadcast([P, NT, NE])
            st.link(v.tensor_tensor(out=pr, in0=bank(4, NT * NE, P).rearrange("p (t e) -> p t e", t=NT),
                                    in1=over_tiles(gb_bc[0:P, :]), op=ALU.add))
            st.link(v.tensor_reduce(out=red[0:P, :], in_=pr, axis=AX.X, op=ALU.max))
            v.tensor_tensor(out=pr, in0=pr, in1=over_experts(red[0:P, :]), op=ALU.subtract).then_inc(lg_sub, 1)
            dve.wait_ge(lg_exp, 1)
            st.link(v.tensor_reduce(out=red[0:P, :], in_=pr, axis=AX.X, op=ALU.add))
            st.link(v.reciprocal(red2[0:P, :], red[0:P, :]))
            st.link(v.tensor_tensor(out=pr, in0=pr, in1=over_experts(red2[0:P, :]), op=ALU.mult))
            pe_ = pr.unsqueeze(3).to_broadcast([P, NT, NE, NE])
            pf = pr.unsqueeze(2).to_broadcast([P, NT, NE, NE])
            low_ = lowE[0:P, :, :].unsqueeze(1).to_broadcast([P, NT, NE, NE])
            c1v, c2v = cmp1[0:P], cmp2[0:P]
            dve.wait_ge(pool_const, CONST["lowP"])
            v.tensor_tensor(out=c1v, in0=pf, in1=pe_, op=ALU.is_gt)
            st.link(v.tensor_tensor(out=c2v, in0=pf, in1=pe_, op=ALU.is_equal))
            st.link(v.tensor_tensor(out=c2v, in0=c2v, in1=low_, op=ALU.mult))
            st.link(v.tensor_tensor(out=c1v, in0=c1v, in1=c2v, op=ALU.add))
            rk = rank8[0:P, :, :]
            st.link(v.tensor_reduce(out=rk, in_=c1v, axis=AX.X, op=ALU.add))
            for k in range(2):
                v.tensor_scalar(oh2[0:P, k, :, :], rk, float(k), None, ALU.is_equal)
            st.link(v.tensor_scalar(rk, rk, float(TOPK), None, ALU.is_lt))
            st.link(v.tensor_tensor(out=wm[0:P, :, :], in0=pr, in1=rk, op=ALU.mult))
            st.link(v.tensor_scalar(rk, rk, -1.0, None, ALU.add))
            v.tensor_tensor(out=wm[0:P, :, :], in0=wm[0:P, :, :], in1=rk, op=ALU.add).then_inc(routed, 1)
            for k in range(2):
                tmp = cmp1[0:P, :, 0, :] if k == 0 else cmp1[0:P, :, 1, :]
                tmp2 = cmp2[0:P, :, 0, :] if k == 0 else cmp2[0:P, :, 1, :]
                v.tensor_tensor(out=tmp, in0=oh2[0:P, k, :, :], in1=pr, op=ALU.mult)
                st.link(v.tensor_tensor(out=tmp2, in0=oh2[0:P, k, :, :], in1=over_tiles(eiota[0:P, :]), op=ALU.mult))
                v.tensor_reduce(out=g2[0:P, k, :], in_=tmp, axis=AX.X, op=ALU.add)
                st.link(v.tensor_reduce(out=e2[0:P, k, :], in_=tmp2, axis=AX.X, op=ALU.add))
            v.memset(cnt[0:P, :, :, :], 0.0).then_inc(dve_step, 1)
            st.n = st.n + 1
            dve.wait_ge(dve_step, st.n)
            for i in range(2 * NT):
                t, k = i // 2, i % 2
                if i >= 2:
                    dve.wait_ge(cnt_used, i - 1)
                dve.wait_ge(cnt_mm, i + 1)
                row = PS[0:P, 1536 * (i % 2):1536 * (i % 2) + N]
                own = g2[0:P, k, t:t + 1]
                if t:
                    v.tensor_scalar(junk[0:P, i % 2, 0:P * t], row[:, 0:P * t], own, None, ALU.is_ge, ALU.add,
                                    accum_out=cnt[0:P, 0, k, t:t + 1])
                v.tensor_scalar(junk[0:P, i % 2, P * t:N], row[:, P * t:N], own, None, ALU.is_gt, ALU.add,
                                accum_out=cnt[0:P, 1, k, t:t + 1])
                v.scalar_tensor_tensor(out=junk2[0:P, i % 2, :], in0=row[:, P * t:P * t + P], scalar=own, in1=lowP[0:P, :],
                                       op0=ALU.is_equal, op1=ALU.mult,
                                       accum_out=cnt[0:P, 2, k, t:t + 1]).then_inc(cnt_used, 1)
            dve.wait_ge(cnt_used, 2 * NT)
            c = [cnt[0:P, a_, :, :] for a_ in range(3)]
            st.link(v.tensor_tensor(out=c[0], in0=c[0], in1=c[1], op=ALU.add))
            st.link(v.tensor_tensor(out=c[0], in0=c[0], in1=c[2], op=ALU.add))
            kp = keep[0:P, :, :]
            v.tensor_scalar(kp, c[0], float(CAP), None, ALU.is_lt)
            st.link(v.tensor_scalar(e2[0:P, :, :], e2[0:P, :, :], float(CAPP), float(-NO_SLOT), ALU.mult, ALU.add))
            st.link(v.tensor_tensor(out=c[0], in0=c[0], in1=e2[0:P, :, :], op=ALU.add))
            st.link(v.tensor_tensor(out=c[0], in0=c[0], in1=kp, op=ALU.mult))
            v.tensor_scalar(slotI[0:P, :, :], c[0], float(NO_SLOT), None, ALU.add).then_inc(slots_ready, 1)

            def expert(e, par, q, first):
                if not first:
                    dve.wait_ge(er_out[par], q * 16)
                for d in range(KD):
                    dve.wait_ge(dn_mm, e * KD + d + 1)
                    if not (first and par == 0 and d < 2):
                        dve.wait_ge(y_T, e * KD + d - 1)
                    v.tensor_scalar(yT[:, d % 2, :], bank(4 + d % 2, CAPP), vcols[:, ds(e * KD + d, 1)], None,
                                    ALU.add).then_inc(y_ready, 1)
                    if d >= 1:
                        rows_out(e, par, d - 1)
                rows_out(e, par, KD - 1)

            def rows_out(e, par, d):
                dve.wait_ge(y_T, e * KD + d + 1)
                v.tensor_copy(er[0:TS, par, :, 128 * d:128 * d + 128],
                              bank(6 + d % 2, 256, TS).rearrange("p (t n) -> p t n", t=2)).then_inc(er_ready, 1)
            expert(0, 0, 0, True)
            expert(1, 1, 0, True)
            with dve.Fori(1, NE // 2) as q:
                for par in range(2):
                    expert(q * 2 + par, par, q, False)
            for i in range(2 * NT):
                t, k = i // 2, i % 2
                dve.wait_ge(fetched[i % 4], 16 * (i // 4 + 1))
                ins = v.scalar_tensor_tensor(out=x2[0:P, t, :], in0=grow[0:P, i % 4, :], scalar=g2[0:P, k, t:t + 1],
                                             in1=x2[0:P, t, :], op0=ALU.mult, op1=ALU.add)
                if k == 0:
                    st.link(ins)
                else:
                    ins.then_inc(sum_ready, 1)

        @block.tensor
        def _(pe):
            te = nc.tensor
            pe.sem_inc(oh_free, GC)
            pe.sem_inc(sel_used, 1)
            pe.wait_ge(pool_const, CONST["ones"])

            def transpose(o, i_, n, k=None):
                return te.transpose(o, i_, identF[0:n, 0:n])
            pe.wait_ge(edge_f, 1)
            for i in range(4):
                ins = transpose(bank(0, CR, CE, CR * i), edgeF[0:CR, i, :], CR)
            ins.then_inc(edge_T, 1)
            pe.wait_ge(g_cols, 1)
            te.matmul(bank(1, 2 * NG, NT), ones[0:NG, 0:NT], gdiag[0:NG, :, :].rearrange("p a g -> p (a g)"),
                      start=True, stop=True).then_inc(g_bc, 1)
            pe.wait_ge(l_v1, 16)
            transpose(bank(2, 128), vrow, 128).then_inc(v_T, 1)
            pe.wait_ge(l_v2, 48)
            transpose(bank(2, 48, 128, 128), vrow2[0:48, :], 48).then_inc(v_T, 1)
            pe.wait_ge(l_v3, 16)
            for k in range(KD):
                ins = transpose(bank(2, NE, 128, 256 + NE * k), vrow3[0:NE, 128 * k:128 * k + 128], NE)
            ins.then_inc(v_T, 1)
            pe.wait_ge(pool_const, CONST["tri10"])
            pe.wait_ge(g_rows, 1)
            eye = identF[0:NT, 0:NT]
            te.matmul(bank(1, NT, 1, 128), bnd[0:NT, 2:3], tri10[0:NT, 0:NT], start=True, stop=True)
            te.matmul(bank(1, NT, 1, 128 + NT), bnd[0:NT, 2:3], tri10[0:NT, 0:NT], start=True, stop=False)
            te.matmul(bank(1, NT, 1, 128 + NT), bnd[0:NT, 2:3], eye, start=False, stop=True)
            te.matmul(bank(1, NT, 1, 128 + 2 * NT), bnd[0:NT, 0:1], eye, start=True, stop=False)
            te.matmul(bank(1, NT, 1, 128 + 2 * NT), bnd[0:NT, 3:4], tri10[0:NT, 0:NT], start=False,
                      stop=True).then_inc(g_rows, 1)
            for t in range(NT):
                pe.wait_ge(xn_ready, t + 1)
                if t >= 2:
                    pe.wait_ge(xnT_ready, t - 1)
                for k in range(KD):
                    ins = transpose(bank(6 + t % 2, P, 128, P * k), xs[0:P, t, 128 * k:128 * k + 128], P)
                ins.then_inc(xn_T, 1)

            pe.wait_ge(pool_const, CONST["wideI"])
            pe.wait_ge(g_ready, 1)
            pe.wait_ge(edge_cols, 1)
            pe.wait_ge(v_cols, 3)
            COLS = ((0, 512), (512, 1024), (1024, N))

            def counts(t, par, first):
                if not first:
                    pe.wait_ge(ctmp_ready, t - 1)
                lo = pe.value_load(bndI[0:1, ds(t, 1)], min_val=0, max_val=NG * NT)
                hi = pe.value_load(bndI[0:1, ds(t + NT, 1)], min_val=1, max_val=NG * NT)
                for c, (a0, a1) in enumerate(COLS):
                    te.matmul(bank(3 * par + c, a1 - a0, P), identB[0:P, 0:P],
                              wideI[0:P, ds(N - P - t * P + a0, a1 - a0)], start=True, stop=False)
                with pe.Fori(lo, hi) as r:
                    for k in range(GC):
                        n = r * GC + k
                        pe.wait_ge(oh_ready, n + 1)
                        for c, (a0, a1) in enumerate(COLS):
                            ins = te.matmul(bank(3 * par + c, a1 - a0, P), ohD[0:CE, k, 0:P], ohS[0:CE, k, a0:a1],
                                            start=False, stop=False)
                        ins.then_inc(oh_free, 1)
                for c in range(3):
                    ins = te.matmul(bank(3 * par + c, 1, P), wideI[0:P, 0:P], wideI[0:P, 0:1], start=False, stop=True)
                ins.then_inc(c_done, 1)

            def counts_T(t, par, first=False):
                pe.wait_ge(ctmp_ready, t + 1)
                for q in range(3):
                    if q == 2:
                        pe.wait_ge(ct_ready, 3 * t + 1)
                    elif q == 0 and not first:
                        pe.wait_ge(ct_ready, 3 * t)
                    for b in range((4, 4, 2)[q]):
                        j = 4 * q + b
                        ins = transpose(bank(6 + q % 2, P, P, P * b), ctmp[0:P, par, P * j:P * j + P], P)
                    ins.then_inc(c_T, 1)
            pe.wait_ge(xnT_ready, NT)
            counts(0, 0, True)
            counts(1, 1, True)
            counts_T(0, 0, True)
            with pe.Fori(1, NT // 2) as q:
                for par in range(2):
                    counts(q * 2 + par, par, False)
                    counts_T(q * 2 + par - 1, 1 - par)
            counts_T(NT - 1, 1)

            def layer(l):
                K = (KD, KC)[l]
                F = (xnT, featT)[l]
                Wl = (W1s, W2s)[l]
                if l == 0:
                    pe.wait_ge(watt_used, 2 * KD)
                    pe.wait_ge(ct_ready, 3 * NT)
                    pe.wait_ge(l_W1, 16)
                else:
                    pe.wait_ge(side_out, SIDES)
                    pe.wait_ge(o_norm, 2 * HEADS)
                    pe.wait_ge(l_W2, 16)
                pe.wait_ge(pool_const, CONST["sel"])
                for c, (a0, a1) in enumerate(COLS):
                    for k in range(K):
                        ins = te.matmul(bank(c, a1 - a0, 8), wa[l][:, k, :], F[:, k, a0:a1], start=k == 0, stop=k == K - 1)
                ins.then_inc(rows_mm, 1)
                pe.wait_ge(rows_ready, l + 1)
                for t in range(NT):
                    ins = te.transpose(bank(6, 8, P, 8 * t), rowsA[:, P * t:P * t + P], identF[0:8, 0:8])
                ins.then_inc(cols_T, 1)

                def spread(h):
                    if h >= 2:
                        pe.wait_ge(m_tile, (HEADS * l + h - 1) * NT)
                    for c, (a0, a1) in enumerate(COLS):
                        ins = te.matmul(bank(3 * (h % 2) + c, a1 - a0, P), sel[:, h, :], rowsA[:, a0:a1], start=True, stop=True)
                    ins.then_inc(mbc, 1)
                spread(0)
                spread(1)
                pe.wait_ge(cols_ready, l + 1)
                for t in range(NT):
                    for c in range(2):
                        n = 2 * NT * l + 2 * t + c
                        if n >= 2:
                            pe.wait_ge(h_ready, n - 1)
                        for k in range(K):
                            ins = te.matmul(bank(6 + c, 512, P), F[:, k, P * t:P * t + P], Wl[:, k, 512 * c:512 * c + 512],
                                            start=k == 0, stop=k == K - 1)
                        ins.then_inc(h_mm, 1)
                    if t == (2, 1)[l]:
                        spread(2)
                    if t == (5, 3)[l]:
                        spread(3)
                pe.wait_ge(r_cols, l + 1)
                for t in range(NT):
                    ins = transpose(bank(t // 4, P, 8, P * (t % 4)), rr[0:P, t, :], P)
                ins.then_inc(r_T, 1)
                pe.wait_ge(rowsR_ready, 3 * (l + 1))
                pe.wait_ge(h_ready, 2 * NT * (l + 1))
                s0 = SIDES * l

                def side(n, kind, half, first=False):
                    if not first:
                        pe.wait_ge(side_out, n)
                    if kind < 2:
                        for a0, a1 in ((0, 512), (512, HALF)):
                            ins = te.matmul(PS[0:P, 2560 + a0:2560 + a1], selcur[:, kind, :],
                                            rowsR[:, HALF * half + a0:HALF * half + a1], start=True, stop=True)
                        ins.then_inc(side_mm, 1)
                    else:
                        for it in range(5):
                            ins = transpose(PS[:, 2560 + 128 * it:2560 + 128 * it + P],
                                            osum[0:P, it, 128 * (kind - 2):128 * (kind - 1)], P)
                        ins.then_inc(side_mm, 1)

                def heads_sel(h):
                    pe.wait_ge(sel_cur, 2 * (h + 1) + 2 * (HEADS + 1) * l)

                def half_body(h, half, first, second=False):
                    u = 2 * h + half
                    b = 2 * HEADS * l + u
                    for j in range(NT):
                        pe.wait_ge(p_ready, b * NT + j + 1)
                        for it in range(5):
                            if j == 0 and not (first and l == 0):
                                if it % 2:
                                    pe.wait_ge(o_act, 2 * b - 1 + it // 2)
                                else:
                                    pe.wait_ge(o_dve, 3 * b - 2 + it // 2)
                            ins = te.matmul(bank(it, HX, P), pring[0:P, j % RING, P * it:P * it + P],
                                            hx[0:P, j, ds(h, 1), :].rearrange("p a c -> p (a c)"),
                                            start=j == 0, stop=j == NT - 1)
                            if j == NT - 1:
                                ins.then_inc(sums, 1)
                        if j < NT - 1:
                            ins.then_inc(p_used, 1)
                        if j in (1, 3):
                            n = s0 + 4 * u + j // 2 + (2 if first else 0)
                            if half == 1 and j == 1:
                                heads_sel(h + 1)
                            side(n, j // 2, 1 - half)
                            if half == 0 and j == 3:
                                pe.wait_ge(side_mm, n + 1)
                                pe.sem_inc(sel_used, 1)
                        if j in (5, 7) and not first:
                            if j == 5:
                                pe.wait_ge(o_norm, b)
                            side(s0 + 4 * u + j // 2, j // 2, 1 - half)
                heads_sel(0)
                side(s0, 0, 0, first=l == 0)
                side(s0 + 1, 1, 0)
                half_body(0, 0, True)
                half_body(0, 1, False, True)
                with pe.Fori(1, HEADS) as h:
                    half_body(h, 0, False)
                    half_body(h, 1, False)
                pe.wait_ge(side_mm, s0 + 8 * HEADS)
                pe.sem_inc(sel_used, 1)
                pe.wait_ge(o_norm, 2 * HEADS * (l + 1))
                side(s0 + 8 * HEADS, 2, 1)
                side(s0 + 8 * HEADS + 1, 3, 1)
            for l in range(2):
                layer(l)

            pe.wait_ge(side_out, 2 * SIDES)
            pe.wait_ge(l_fcW, 16)

            def logits(t):
                pe.wait_ge(xn2_ready, t + 1)
                if t >= 2:
                    pe.wait_ge(xn2T_ready, t - 1)
                for k in range(KD):
                    ins = transpose(bank(2 + t % 2, P, 128, P * k), xn2[0:P, t, 128 * k:128 * k + 128], P)
                ins.then_inc(xn2_T, 1)
                pe.wait_ge(xn2T_ready, t + 1)
                for k in range(KD):
                    ins = te.matmul(bank(4, NE, P, NE * t), xn2T[:, t % 2, k, :], gwT[:, k, :], start=k == 0, stop=k == KD - 1)
                ins.then_inc(lg_mm, 1)
            for t in range(NT):
                if t >= 2:
                    pe.wait_ge(var2, t - 1)
                for k in range(KC):
                    ins = te.matmul(bank(t % 2, D, P), featT[:, k, P * t:P * t + P], fcWs[:, k, :], start=k == 0, stop=k == KC - 1)
                ins.then_inc(fc_mm, 1)
                if t:
                    logits(t - 1)
            logits(NT - 1)
            pe.wait_ge(routed, 1)
            for k in range(3):
                src_ = wm[0:P, :, :] if k == 0 else oh2[0:P, k - 1, :, :]
                if k == 2:
                    pe.wait_ge(rt_rows, 3)
                for t in range(NT):
                    ins = transpose(bank(3 * (k % 2) + t // 4, P, 8, P * (t % 4)), src_[:, t, :], P)
                ins.then_inc(rt_T, 1)
            pe.wait_ge(rt_rows, 9)
            for i in range(2 * NT):
                t, k = i // 2, i % 2
                if i >= 2:
                    pe.wait_ge(cnt_used, i - 1)
                for c, (a0, a1) in enumerate(COLS):
                    ins = te.matmul(bank(3 * (i % 2) + c, a1 - a0, P), ohT[0:8, k, P * t:P * t + P], wmT[0:8, a0:a1],
                                    start=True, stop=True)
                ins.then_inc(cnt_mm, 1)
            pe.wait_ge(cnt_used, 2 * NT)

            def expert(e, par, q, first):
                pe.wait_ge(xr_in[par], q * 16 + 16)
                for b in range(2):
                    if not (first and par == 0):
                        pe.wait_ge(xgT_ready, 2 * e - 1 + b)
                    for k in (2 * b, 2 * b + 1):
                        for t in range(2):
                            ins = transpose(bank(b, TS, 128, CAPP * (k % 2) + TS * t), xr[0:TS, par, t, 128 * k:128 * k + 128], TS)
                    ins.then_inc(xg_T, 1)
                pe.wait_ge(xgT_ready, 2 * e + 2)
                pe.wait_ge(w1_in[par], q * 16 + 16)
                for m in range(FM):
                    if not (first and par == 0 and m < 2):
                        pe.wait_ge(up_ready, e * FM + m - 1)
                    for k in range(KD):
                        ins = te.matmul(bank(2 + m % 2, CAPP), w1s[par][:, k, 128 * m:128 * m + 128], xgT[:, par, k, :],
                                        start=k == 0, stop=k == KD - 1)
                    ins.then_inc(up_mm, 1)
                pe.wait_ge(w2_in[par], q * 16 + 16)
                for d in range(KD):
                    if not (first and par == 0 and d < 2):
                        pe.wait_ge(y_ready, e * KD + d - 1)
                    for m in range(FM):
                        if d == 0:
                            pe.wait_ge(up_ready, e * FM + m + 1)
                        ins = te.matmul(bank(4 + d % 2, CAPP), w2s[par][:, m, 128 * d:128 * d + 128], hT[:, m, :],
                                        start=m == 0, stop=m == FM - 1)
                    ins.then_inc(dn_mm, 1)
                    if d >= 1:
                        y_rows(e, par, d - 1, first)
                y_rows(e, par, KD - 1, first)

            def y_rows(e, par, d, first):
                pe.wait_ge(y_ready, e * KD + d + 1)
                if not (first and par == 0 and d < 2):
                    pe.wait_ge(er_ready, e * KD + d - 1)
                for t in range(2):
                    ins = te.transpose(bank(6 + d % 2, 128, TS, 128 * t), yT[:, d % 2, TS * t:TS * t + TS], identF[:, :])
                ins.then_inc(y_T, 1)
            expert(0, 0, 0, True)
            expert(1, 1, 0, True)
            with pe.Fori(1, NE // 2) as q:
                for par in range(2):
                    expert(q * 2 + par, par, q, False)


_INS = ["x", "src", "dst", "L0_gnn_W1", "L0_gnn_att_src1", "L0_gnn_att_dst1", "L0_gnn_b1", "L0_gnn_W2",
        "L0_gnn_att_src2", "L0_gnn_att_dst2", "L0_gnn_b2", "L0_gnn_fcW", "L0_gnn_fcb", "L0_ffn_gate_w",
        "L0_ffn_gate_b", "L0_ffn_w1", "L0_ffn_b1", "L0_ffn_w2", "L0_ffn_b2"]


def kernel(**inputs):
    import concourse.bacc as _bacc
    from concourse.bass_utils import run_bass_kernel_spmd as _run

    nc = _bacc.Bacc("TRN2", target_bir_lowering=False, num_devices=1)
    arrays, args = {}, []
    for name in _INS:
        a = np.ascontiguousarray(inputs[name])
        arrays["in_" + name] = a
        args.append(nc.dram_tensor("in_" + name, a.shape, mybir.dt.from_np(a.dtype), kind="ExternalInput").ap())
    args.append(nc.dram_tensor("out_x", (N, D), mybir.dt.float32, kind="ExternalOutput").ap())
    program(nc, *args)
    return _run(nc, [arrays], core_ids=[0]).results[0]["out_x"]
```

```python
import numpy as np
from contextlib import ExitStack

import concourse.bass as bass
from concourse import mybir
from concourse.bass import ds

N, E = 1250, 20000
D, HEADS, HID, C1 = 512, 4, 256, 1024
NE, TOPK, FF = 8, 2, 2048
CAP = int(1.2 * N / NE)
SLOPE, EPS_LN, EPS_SM = 0.2, 1e-5, 1e-16

P = 125
NT = N // P
HALF = 5 * P
HX = HID + 1
FCB = (7, 0, 1)
CE = 125
NCH = E // CE
CR = NCH // 2
GC = 4
NG = NCH // GC
CAPP = 188
TS = CAPP // 2
SLOTS = NE * CAPP
ROW = D + 4
PARTS = 3 * NE
BIG = 2.0 ** 64
BATCHES = ((0, 5), (5, 8), (8, NT))
NO_SLOT = SLOTS
FM = FF // 128
KD = D // 128
KC = C1 // 128
MASKED = -1e30
RING = 5
SMALL = 1700
SIDE = 5 * 512
SIDES = 8 * HEADS + 2


def program(nc, x, src, dst, W1, as1, ad1, b1, W2, as2, ad2, b2, fcW, fcb,
            gate_w, gate_b, w1, mb1, w2, mb2, out):
    dt, ALU, ACT, AX = mybir.dt, mybir.AluOpType, mybir.ActivationFunctionType, mybir.AxisListType
    f32, bf16, f16, i32, i16 = dt.float32, dt.bfloat16, dt.float16, dt.int32, dt.int16

    xg = nc.dram_tensor("xg", [SLOTS, ROW], f32, kind="Internal").ap()

    with ExitStack() as ctx:
        def sb(name, shape, d=f32):
            return ctx.enter_context(nc.sbuf_tensor(name, shape, d))

        def sem(name):
            return ctx.enter_context(nc.semaphore(name))

        areaA = sb("areaA", [128, NT * HEADS * HX])
        areaB = sb("areaB", [128, KC * N])
        areaC = sb("areaC", [128, NT * N])
        areaW = sb("areaW", [128, KC * C1])

        def view(area, at, n, d=f32):
            size = {f32: 1, i32: 1}.get(d, 2)
            cols = -(-n // size)
            v = area[:, at:at + cols]
            return (v if d == f32 else v.bitcast(d))[:, 0:n], at + cols

        a = 0
        wideI, a = view(areaA, a, 2 * N - P, bf16)
        iotaN, a = view(areaA, a, N, f16)
        edgeT, a = view(areaA, a, 2 * NCH)
        ohS, a = view(areaA, a, GC * N, bf16)
        ohD, a = view(areaA, a, GC * 126, bf16)
        ctmp, a = view(areaA, a, 2 * N)
        edgeI, a = view(areaA, a, 4 * CE, i32)
        edgeF, a = view(areaA, a, 4 * CE)
        grpI, a = view(areaA, a, GC * CE, i32)
        grpF, a = view(areaA, a, GC * CE)
        assert a <= NT * HEADS * HX
        ohS = ohS.rearrange("p (g n) -> p g n", g=GC)
        ohD = ohD.rearrange("p (g n) -> p g n", g=GC)
        ctmp = ctmp.rearrange("p (g n) -> p g n", g=2)
        edgeI = edgeI.rearrange("p (g n) -> p g n", g=4)
        edgeF = edgeF.rearrange("p (g n) -> p g n", g=4)
        hx = areaA[:, :].rearrange("p (t h c) -> p t h c", t=NT, h=HEADS)
        W1s = areaB[:, 0:KD * C1].rearrange("p (k c) -> p k c", k=KD)
        xnT = areaB[:, KD * C1:KD * C1 + KD * N].rearrange("p (k n) -> p k n", k=KD)
        featT = areaB[:, :].rearrange("p (k n) -> p k n", k=KC)
        att2 = areaB[:, 6 * N:6 * N + 2 * C1].rearrange("p (a c) -> p a c", a=2)
        CT, _ = view(areaC, 0, NT * N, i16)
        mask, _ = view(areaC, NT * N // 2, NT * N, bf16)
        CT = CT.rearrange("p (t n) -> p t n", t=NT)
        mask = mask.rearrange("p (t n) -> p t n", t=NT)
        a = 0
        xn2, a = view(areaC, a, NT * ROW)
        xn2 = xn2.rearrange("p (t d) -> p t d", t=NT)
        xn2T, a = view(areaC, a, 2 * KD * P)
        xn2T = xn2T.rearrange("p (b k n) -> p b k n", b=2, k=KD)
        fcb_bc, a = view(areaC, a, D)
        cmp1, a = view(areaC, a, NT * NE * NE)
        cmp2, a = view(areaC, a, NT * NE * NE)
        wmT, a = view(areaC, a, N, bf16)
        ohT, a = view(areaC, a, 2 * N, bf16)
        prob, a = view(areaC, a, NT * NE)
        wm, a = view(areaC, a, NT * NE)
        rank8, a = view(areaC, a, NT * NE)
        oh2, a = view(areaC, a, 2 * NT * PARTS)
        wm3, a = view(areaC, a, NT * PARTS)
        part, a = view(areaC, a, NT * NE, bf16)
        cnt, a = view(areaC, a, 3 * 2 * NT)
        prob, wm, rank8 = [v.rearrange("p (t e) -> p t e", t=NT) for v in (prob, wm, rank8)]
        part = part.rearrange("p (t e) -> p t e", t=NT)
        oh2 = oh2.rearrange("p (k t a e) -> p k t a e", k=2, t=NT, a=3)
        wm3 = wm3.rearrange("p (t a e) -> p t a e", t=NT, a=3)
        cnt = cnt.rearrange("p (a k t) -> p a k t", a=3, k=2)
        assert a <= NT * N
        cmp1 = cmp1.rearrange("p (t a b) -> p t a b", t=NT, a=NE)
        cmp2 = cmp2.rearrange("p (t a b) -> p t a b", t=NT, a=NE)
        ohT = ohT.rearrange("p (k n) -> p k n", k=2)
        xs = areaW[:, 0:NT * D].rearrange("p (t d) -> p t d", t=NT)
        W2s = areaW[:, :].rearrange("p (k c) -> p k c", k=KC)
        fcWs = areaW[:, 0:KC * D].rearrange("p (k c) -> p k c", k=KC)
        WSZ = KD * FF
        w1s = [v[:, 0:WSZ].rearrange("p (k c) -> p k c", k=KD) for v in (areaA, areaB)]
        w2s = [v[:, 0:WSZ].rearrange("p (k c) -> p k c", k=FM) for v in (areaW, areaC)]
        hT = areaC[:, WSZ:WSZ + FM * CAPP].rearrange("p (m n) -> p m n", m=FM)
        xring = areaA[:, WSZ:WSZ + 2 * D].rearrange("p (b d) -> p b d", b=2)
        xgT = areaB[:, WSZ:WSZ + 2 * KD * CAPP].rearrange("p (b k n) -> p b k n", b=2, k=KD)

        work = sb("work", [128, (4 + RING) * HALF + 5 * HX + 512])
        att_bc = work[:, 0:2 * C1].rearrange("p (a c) -> p a c", a=2)
        watt = work[:, 2 * C1:4 * C1].rearrange("p (a c) -> p a c", a=2)
        ring = work[:, 0:(4 + RING) * HALF].rearrange("p (r n) -> p r n", r=4 + RING)
        rbc = [[ring[:, 0], ring[:, 1]], [ring[:, 2], ring[:, 3]]]
        pring = ring[:, 4:4 + RING]
        osum = work[:, (4 + RING) * HALF:(4 + RING) * HALF + 5 * HX].rearrange("p (t c) -> p t c", t=5)
        prod = work[:, (4 + RING) * HALF + 5 * HX:]
        junkb = work[:, (4 + RING) * HALF:(4 + RING) * HALF + N].bitcast(bf16).rearrange("p (b n) -> p b n", b=2)
        x2 = work[:, 0:NT * D].rearrange("p (t d) -> p t d", t=NT)

        identF = sb("identF", [128, 128])
        identB = sb("identB", [128, 128], bf16)
        byhead = sb("byhead", [8, 9 * P + N + 2 * P])
        sel = byhead[0:8, 0:9 * P].rearrange("p (r n) -> p r n", r=9)
        rowsA = byhead[0:8, 9 * P:9 * P + N]
        rowsR = rowsA
        selcur = byhead[0:8, 9 * P + N:].rearrange("p (r n) -> p r n", r=2)
        xr = areaA[:, WSZ:WSZ + 2 * 2 * ROW].rearrange("p (b t d) -> p b t d", b=2, t=2)
        er = work[:, NT * D:NT * D + 2 * 2 * D].rearrange("p (b t d) -> p b t d", b=2, t=2)
        yT = areaC[:, WSZ + FM * CAPP:WSZ + FM * CAPP + 2 * CAPP].rearrange("p (b n) -> p b n", b=2)
        junk = work[:, NT * D:NT * D + N].bitcast(bf16).rearrange("p (b n) -> p b n", b=2)
        junk2 = work[:, NT * D + N:NT * D + N + P].bitcast(bf16).rearrange("p (b n) -> p b n", b=2)
        small = sb("small", [128, SMALL])
        s = 0

        def sm(n, d=f32):
            nonlocal s
            v, s = view(small, s, n, d)
            return v
        wa = [sm(KD * 8).rearrange("p (k r) -> p k r", k=KD), sm(KC * 8).rearrange("p (k r) -> p k r", k=KC)]
        asd = sm(NT * 8).rearrange("p (t r) -> p t r", t=NT)
        as02 = sm(NT * 4).rearrange("p (t r) -> p t r", t=NT)
        mx = sm(NT * 4).rearrange("p (t r) -> p t r", t=NT)
        mlk = sm(NT * 4).rearrange("p (t r) -> p t r", t=NT)
        rr = sm(NT * 8).rearrange("p (t r) -> p t r", t=NT)
        stat = sm(NT * 6).rearrange("p (t r) -> p t r", t=NT)
        mv = sm(NT * 2).rearrange("p (t r) -> p t r", t=NT)
        sd = sm(NT)
        rstd = sm(NT)
        rsum = sm(10).rearrange("p (t r) -> p t r", t=2)
        b1cols = sm(128)
        vcols = sm(48)
        gwT = sm(KD * NE).rearrange("p (k e) -> p k e", k=KD)
        gb_bc = sm(NE)
        ones = sm(128)
        gmm = sm(2)
        gdiag = sm(2 * NG).rearrange("p (a g) -> p a g", a=2)
        tlo = sm(1)
        thi = sm(1)
        gup = sm(NG)
        gdn = sm(NG)
        hit = sm(NG)
        hit2 = sm(NG)
        hitv = sm(2 * NG).rearrange("p (a g) -> p a g", a=2)
        bnd = sm(4)
        tri10 = sm(NT)
        bndI = sm(3 * NT, i32)
        red = sm(NT)
        red2 = sm(NT)
        eiota = sm(NE)
        lowE = sm(NE * NE).rearrange("p (a b) -> p a b", a=NE)
        lowP = sm(P)
        g2 = sm(2 * NT).rearrange("p (k t) -> p k t", k=2)
        e2 = sm(2 * NT).rearrange("p (k t) -> p k t", k=2)
        keep = sm(2 * NT).rearrange("p (k t) -> p k t", k=2)
        g2big = sm(2 * NT).rearrange("p (k t) -> p k t", k=2)
        idxI = sm(4, i32).rearrange("p (b t) -> p b t", b=2)
        gate = sm(8).rearrange("p (b t) -> p b t", b=4)
        slotI = sm(2 * NT, i32).rearrange("p (k t) -> p k t", k=2)
        assert s <= SMALL, s
        vrow = areaA[:, 9400:9400 + 128]
        vrow2 = areaA[:, 9528:9528 + 128]
        vrow3 = areaA[:, 9656:9656 + D]
        zrow = areaC[:, 0:12 * ROW].rearrange("p (t d) -> p t d", t=12)

        PS = ctx.enter_context(nc.psum_tensor("PS", [128, 8 * 512], f32))

        def bank(b, n=512, p=128, at=0):
            return PS[0:p, 512 * b + at:512 * b + at + n]

        (l_edge, l_grp, l_x, l_W1, l_att0, l_att1, l_W2, l_fcW, l_v1, l_v2, l_v3, l_fcb, l_gb, l_zero,
         l_outs) = [sem("l_" + n) for n in
                    "edge grp x W1 att0 att1 W2 fcW v1 v2 v3 fcb gb zero outs".split()]
        l_xr = [sem("l_x0"), sem("l_x1")]
        (pool_const, edge_f, grp_f, edge_T, edge_cols, g_bc, g_cols, g_rows, g_ready, v_T, v_cols) = [
            sem(n) for n in ("pool_const edge_f grp_f edge_T edge_cols g_bc g_cols g_rows g_ready v_T v_cols").split()]
        var_eps, std, xn_ready, xn_T, xnT_ready = [sem(n) for n in "var_eps std xn_ready xn_T xnT_ready".split()]
        oh_ready, oh_free, c_done, ctmp_ready, mask_ready, c_T, ct_ready = [
            sem(n) for n in "oh_ready oh_free c_done ctmp_ready mask_ready c_T ct_ready".split()]
        watt_ready, watt_used, wa_ready = [sem(n) for n in "watt_ready watt_used wa_ready".split()]
        rows_mm, rows_ready, cols_T, cols_ready, mbc, m_tile, h_mm, h_ready, r_cols, r_T, rowsR_ready = [
            sem(n) for n in
            "rows_mm rows_ready cols_T cols_ready mbc m_tile h_mm h_ready r_cols r_T rowsR_ready".split()]
        sel_cur, sel_used, side_mm, side_out, low_ready, top_ready, exp_ready, p_ready, p_used, sums, o_dve, \
            o_act, o_norm = [sem(n) for n in
                             "sel_cur sel_used side_mm side_out low_ready top_ready exp_ready p_ready p_used "
                             "sums o_dve o_act o_norm".split()]
        fc_mm, x2b, x2_ready, xr_used = [sem(n) for n in "fc_mm x2b x2_ready xr_used".split()]
        var2, std2, xn2_ready, xn2_T, xn2T_ready, lg_mm, lg_sub, lg_exp = [
            sem(n) for n in "var2 std2 xn2_ready xn2_T xn2T_ready lg_mm lg_sub lg_exp".split()]
        routed, rt_T, rt_rows, cnt_mm, cnt_used, slots_ready, scat = [
            sem(n) for n in "routed rt_T rt_rows cnt_mm cnt_used slots_ready scat".split()]
        w1_in = [sem("w1_in0"), sem("w1_in1")]
        w2_in = [sem("w2_in0"), sem("w2_in1")]
        xr_in = [sem("xr_in0"), sem("xr_in1")]
        xg_T, xgT_ready, up_mm, up_ready, dn_mm, y_ready, y_T, er_ready = [
            sem(n) for n in "xg_T xgT_ready up_mm up_ready dn_mm y_ready y_T er_ready".split()]
        er_out = sem("er_out")
        er_in = [sem("er_in0"), sem("er_in1")]
        er_zero, idx_ready, meta_step, gate_ready, s_eps, s_inv = [
            sem(n) for n in "er_zero idx_ready meta_step gate_ready s_eps s_inv".split()]
        settled = sem("settled")
        zeros_ready = sem("zeros_ready")
        CONST = {n: i + 1 for i, n in enumerate("ones tlo thi gup gdn eiota iotaN tri10 identB wideI lowE lowP sel hx number".split())}
        dve_step, act_step, pool_step = sem("dve_step"), sem("act_step"), sem("pool_step")

        class Steps:
            def __init__(self, eng, sm_):
                self.eng, self.sem, self.n = eng, sm_, 0

            def link(self, ins):
                ins.then_inc(self.sem, 1)
                self.n = self.n + 1
                self.eng.wait_ge(self.sem, self.n)

        def settle(eng):
            eng.sem_inc(settled, 1)

        block = ctx.enter_context(nc.Block())

        @block.sync
        def _(sp):
            sp.dma_start(edgeI[0:CR, 0:2, :], src.rearrange("(r p k) -> p r k", r=2, p=CR)).then_inc(l_edge, 16)
            sp.dma_start(edgeI[0:CR, 2:4, :], dst.rearrange("(r p k) -> p r k", r=2, p=CR)).then_inc(l_edge, 16)
            sp.dma_start(grpI[0:NG, :], dst.rearrange("(g k) -> g k", g=NG)).then_inc(l_grp, 16)
            sp.dma_start(xs[0:P, :, :], x.rearrange("(t p) d -> p t d", p=P)).then_inc(l_x, 16)
            sp.dma_start(W1s[:, :, :], W1.rearrange("(k p) c -> p k c", p=128)).then_inc(l_W1, 16)
            sp.dma_start(vrow, mb1.rearrange("e (m p) -> (e m) p", p=128)).then_inc(l_v1, 16)
            sp.dma_start(vrow2[0:32, :], mb2.rearrange("e (m p) -> (e m) p", p=128)).then_inc(l_v2, 16)
            sp.dma_start(vrow2[32:40, :], b1.rearrange("(m p) -> m p", p=128)).then_inc(l_v2, 16)
            sp.dma_start(vrow2[40:48, :], b2.rearrange("(m p) -> m p", p=128)).then_inc(l_v2, 16)
            sp.dma_start(vrow3[0:NE, :], gate_w).then_inc(l_v3, 16)
            sp.dma_start(gb_bc[0:P, :], gate_b.rearrange("(a e) -> a e", a=1).to_broadcast([P, NE])).then_inc(l_gb, 16)
            sp.wait_ge(zeros_ready, 1)
            sp.dma_start(xg[0:12 * 124, :].rearrange("(p t) d -> p t d", t=12), zrow[0:124, :, :]).then_inc(l_zero, 16)
            sp.dma_start(xg[12 * 124:SLOTS, :], zrow[0:SLOTS - 12 * 124, 0, :]).then_inc(l_zero, 16)
            sp.wait_ge(xn_T, NT)
            sp.dma_start(W2s[:, :, :], W2.rearrange("(k p) c -> p k c", p=128)).then_inc(l_W2, 16)
            sp.wait_ge(h_mm, 2 * 2 * NT)
            sp.dma_start(fcWs[:, :, :], fcW.rearrange("(k p) c -> p k c", p=128)).then_inc(l_fcW, 16)
            sp.wait_ge(sums, 5 * 2 * 2 * HEADS)
            sp.dma_start(fcb_bc[0:P, :], fcb.rearrange("(a e) -> a e", a=1).to_broadcast([P, D])).then_inc(l_fcb, 16)
            for t in range(NT):
                if t >= 2:
                    sp.wait_ge(xr_used, t - 1)
                sp.dma_start(xring[0:P, t % 2, :], x[P * t:P * t + P, :]).then_inc(l_xr[t % 2], 16)

            w1_v = w1.rearrange("e (k p) c -> e p k c", p=128)
            w2_v = w2.rearrange("e (k p) c -> e p k c", p=128)
            sp.dma_start(w1s[0][:, :, :], w1_v[0]).then_inc(w1_in[0], 16)
            sp.wait_ge(fc_mm, NT)
            sp.dma_start(w2s[0][:, :, :], w2_v[0]).then_inc(w2_in[0], 16)
            sp.dma_start(w1s[1][:, :, :], w1_v[1]).then_inc(w1_in[1], 16)
            for t in range(NT):
                sp.wait_ge(var2, t + 1)
                sp.dma_start(out[P * t:P * t + P, :], x2[0:P, t, :]).then_inc(l_outs, 16)
            sp.wait_ge(scat, 16 * 2 * NT)

            def load_rows(e, par):
                sp.dma_start(xr[0:TS, par, :, :],
                             xg[ds(e * CAPP, CAPP), :].rearrange("(t p) d -> p t d", p=TS)).then_inc(xr_in[par], 16)
            load_rows(0, 0)
            load_rows(1, 1)
            sp.dma_start(w2s[1][:, :, :], w2_v[1]).then_inc(w2_in[1], 16)
            with sp.Fori(0, NE // 2 - 1) as q:
                for par in range(2):
                    e = q * 2 + par
                    sp.wait_ge(gate_ready, e + 1)
                    settle(sp)
                    sp.wait_ge(xg_T, 2 * e + 2)
                    settle(sp)
                    load_rows(e + 2, par)
                    sp.wait_ge(up_mm, FM * e + FM)
                    sp.dma_start(w1s[par][:, :, :], w1_v[ds(e + 2, 1)].rearrange("a p k c -> p (a k) c")).then_inc(w1_in[par], 16)
                    sp.wait_ge(dn_mm, 4 * e + 4)
                    sp.dma_start(w2s[par][:, :, :], w2_v[ds(e + 2, 1)].rearrange("a p k c -> p (a k) c")).then_inc(w2_in[par], 16)

        @block.gpsimd
        def _(pool):
            st = Steps(pool, pool_step)
            g = nc.gpsimd
            st.link(g.memset(identF[:], 0.0))
            st.link(g.affine_select(out=identF[:], in_=identF[:], compare_op=ALU.not_equal, fill=1.0, base=0,
                                    pattern=[[-1, 128]], channel_multiplier=1))
            g.memset(ones[:], 1.0).then_inc(pool_const, 1)
            g.iota(tlo[0:NT, :], pattern=[[0, 1]], base=0, channel_multiplier=P,
                   allow_small_or_imprecise_dtypes=True).then_inc(pool_const, 1)
            g.iota(thi[0:NT, :], pattern=[[0, 1]], base=P - 1, channel_multiplier=P,
                   allow_small_or_imprecise_dtypes=True).then_inc(pool_const, 1)
            g.iota(gup[0:NT, :], pattern=[[1, NG]], base=1, channel_multiplier=0,
                   allow_small_or_imprecise_dtypes=True).then_inc(pool_const, 1)
            g.iota(gdn[0:NT, :], pattern=[[-1, NG]], base=NG, channel_multiplier=0,
                   allow_small_or_imprecise_dtypes=True).then_inc(pool_const, 1)
            g.iota(eiota[:, :], pattern=[[1, NE]], base=0, channel_multiplier=0,
                   allow_small_or_imprecise_dtypes=True).then_inc(pool_const, 1)
            g.iota(iotaN[:, :], pattern=[[1, N]], base=0, channel_multiplier=0,
                   allow_small_or_imprecise_dtypes=True).then_inc(pool_const, 1)
            st.link(g.memset(tri10[0:NT, :], 1.0))
            g.affine_select(out=tri10[0:NT, :], in_=tri10[0:NT, :], compare_op=ALU.is_gt, fill=0.0, base=0,
                            pattern=[[1, NT]], channel_multiplier=-1).then_inc(pool_const, 1)
            g.tensor_copy(identB[:], identF[:]).then_inc(pool_const, 1)
            g.memset(zrow[:, :, :], 0.0).then_inc(zeros_ready, 1)
            st.link(g.memset(wideI[:, :], 0.0))
            g.affine_select(out=wideI[:, :], in_=wideI[:, :], compare_op=ALU.not_equal, fill=1.0, base=N - P,
                            pattern=[[-1, 2 * N - P]], channel_multiplier=1).then_inc(pool_const, 1)
            st.link(g.memset(lowE[:, :, :], 1.0))
            g.affine_select(out=lowE[:, :, :], in_=lowE[:, :, :], compare_op=ALU.is_gt, fill=0.0, base=0,
                            pattern=[[1, NE], [-1, NE]], channel_multiplier=0).then_inc(pool_const, 1)
            st.link(g.memset(lowP[:, :], 1.0))
            g.affine_select(out=lowP[:, :], in_=lowP[:, :], compare_op=ALU.is_gt, fill=0.0, base=0,
                            pattern=[[-1, P]], channel_multiplier=1).then_inc(pool_const, 1)
            st.link(g.memset(sel[:, :, :], 0.0))
            g.affine_select(out=sel[:, :, :], in_=sel[:, :, :], compare_op=ALU.not_equal, fill=1.0, base=0,
                            pattern=[[-1, 9], [0, P]], channel_multiplier=1).then_inc(pool_const, 1)

            for i, av in enumerate((as1, ad1)):
                pool.dma_start(att_bc[:, i, :], av.rearrange("(a h) c -> a (h c)", a=1).to_broadcast([128, C1]))\
                    .then_inc(l_att0, 16)
            pool.wait_ge(l_att0, 32)
            pool.wait_ge(l_W1, 16)
            for k in range(KD):
                for i in range(2):
                    n = 2 * k + i
                    if n >= 2:
                        pool.wait_ge(watt_used, n - 1)
                    g.tensor_tensor(out=watt[:, i, :], in0=W1s[:, k, :], in1=att_bc[:, i, :],
                                    op=ALU.mult).then_inc(watt_ready, 1)
            pool.wait_ge(c_T, 3 * NT)
            pool.wait_ge(v_cols, 3)
            pool.wait_ge(mask_ready, NT)
            g.memset(hx[:, :, :, HID:HX], 1.0).then_inc(pool_const, 1)

            def select_head(l, h):
                pool.wait_ge(sel_used, h + l * (HEADS + 1) + 1)
                for i in range(2):
                    ins = g.tensor_copy(selcur[:, i, :], sel[:, ds(h + 4 * i, 1), :].rearrange("p a n -> p (a n)"))
                    ins.then_inc(sel_cur, 1)

            def products(k):
                for q in range(4):
                    i, c = q // 2, q % 2
                    pool.wait_ge(watt_used, 2 * KD + 4 * k + q)
                    settle(pool)
                    g.tensor_tensor(out=prod, in0=W2s[:, ds(k, 1), 512 * c:512 * c + 512].rearrange("p a n -> p (a n)"),
                                    in1=att2[:, i, 512 * c:512 * c + 512], op=ALU.mult).then_inc(watt_ready, 1)
            select_head(0, 0)
            pool.wait_ge(h_mm, 2 * NT)
            for i, av in enumerate((as2, ad2)):
                pool.dma_start(att2[:, i, :], av.rearrange("(a h) c -> a (h c)", a=1).to_broadcast([128, C1]))\
                    .then_inc(l_att1, 16)
            pool.wait_ge(l_att1, 32)
            pool.wait_ge(l_W2, 16)
            products(0)
            select_head(0, 1)
            with pool.Fori(1, HEADS) as h:
                products(h * 2 - 1)
                products(h * 2)
                select_head(0, h + 1)
            products(KC - 1)
            with pool.Fori(0, HEADS + 1) as h:
                select_head(1, h)
            pool.wait_ge(l_fcb, 16)
            pool.wait_ge(side_mm, 2 * SIDES)
            for t in range(NT):
                pool.wait_ge(l_xr[t % 2], 16 * (t // 2 + 1))
                g.tensor_tensor(out=x2[0:P, t, :], in0=xring[0:P, t % 2, :], in1=fcb_bc[0:P, :],
                                op=ALU.add).then_inc(xr_used, 1)
            g.iota(xn2[0:P, :, D:D + 1], pattern=[[-P, NT], [0, 1]], base=N, channel_multiplier=-1,
                   allow_small_or_imprecise_dtypes=True).then_inc(pool_const, 1)
            pool.wait_ge(l_zero, 32)
            for n, (t0, t1) in enumerate(BATCHES):
                pool.wait_ge(slots_ready, n + 1)
                for t in range(t0, t1):
                    for k in range(2):
                        g.indirect_dma_start(out=xg, out_offset=bass.IndirectOffsetOnAxis(ap=slotI[0:P, k, t:t + 1], axis=0),
                                             in_=xn2[0:P, t, :], in_offset=None,
                                             bounds_check=SLOTS - 1, oob_is_err=False).then_inc(scat, 16)
            g.memset(er[0:TS, :, :, :], 0.0).then_inc(er_zero, 1)
            pool.wait_ge(er_zero, 1)
            pool.wait_ge(l_outs, 16 * NT)

            def add_rows(e, par, first):
                pool.wait_ge(idx_ready, e + 1)
                if not first:
                    pool.wait_ge(er_out, e * 32)
                settle(pool)
                for t in range(2):
                    g.indirect_dma_start(out=er[0:TS, par, t, :], out_offset=None, in_=out,
                                         in_offset=bass.IndirectOffsetOnAxis(ap=idxI[0:TS, par, t:t + 1], axis=0),
                                         bounds_check=N - 1, oob_is_err=False).then_inc(er_in[par], 16)
                pool.wait_ge(er_ready, e * KD + KD)
                settle(pool)
                for t in range(2):
                    g.indirect_dma_start(out=out, out_offset=bass.IndirectOffsetOnAxis(ap=idxI[0:TS, par, t:t + 1], axis=0),
                                         in_=er[0:TS, par, t, :], in_offset=None,
                                         bounds_check=N - 1, oob_is_err=False).then_inc(er_out, 16)
            add_rows(0, 0, True)
            add_rows(1, 1, False)
            with pool.Fori(1, NE // 2) as q:
                for par in range(2):
                    add_rows(q * 2 + par, par, False)
            pool.wait_ge(er_out, 32 * NE)

        @block.scalar
        def _(act):
            sc = nc.scalar

            act.wait_ge(var_eps, 1)
            sc.activation(sd[0:P, :], sd[0:P, :], ACT.Sqrt).then_inc(std, 1)
            for t in range(NT):
                act.wait_ge(xn_T, t + 1)
                sc.activation(xnT[:, :, P * t:P * t + P],
                              bank(6 + t % 2, KD * P).rearrange("p (k n) -> p k n", k=KD), ACT.Copy).then_inc(xnT_ready, 1)

            def counts_out(t, par, first):
                act.wait_ge(c_done, t + 1)
                if not first:
                    act.wait_ge(c_T, 3 * t - 3)
                    act.wait_ge(mask_ready, t - 1)
                sc.activation(ctmp[0:P, par, :], PS[0:P, 1536 * par:1536 * par + N], ACT.Copy).then_inc(ctmp_ready, 1)

            def counts_T_out(t, par):
                for q in range(3):
                    b = (4, 4, 2)[q]
                    act.wait_ge(c_T, 3 * t + q + 1)
                    sc.activation(CT[0:P, 4 * q:4 * q + b, ds(t * P, P)],
                                  bank(6 + q % 2, b * P, P).rearrange("p (b n) -> p b n", b=b),
                                  ACT.Copy).then_inc(ct_ready, 1)
            act.wait_ge(l_zero, 32)
            counts_out(0, 0, True)
            counts_out(1, 1, True)
            counts_T_out(0, 0)
            with act.Fori(1, NT // 2) as q:
                for par in range(2):
                    counts_out(q * 2 + par, par, False)
                    counts_T_out(q * 2 + par - 1, 1 - par)
            counts_T_out(NT - 1, 1)

            def layer(l):
                def h_out(l_, t, c):
                    n = 2 * NT * l_ + 2 * t + c
                    act.wait_ge(h_mm, n + 1)
                    if n == 0:
                        act.wait_ge(pool_const, CONST["hx"])
                    sc.activation(hx[0:P, t, 2 * c:2 * c + 2, 0:HID],
                                  bank(7 - c, 512, P).rearrange("p (h n) -> p h n", h=2), ACT.Copy).then_inc(h_ready, 1)
                if l:
                    h_out(1, 0, 1)
                act.wait_ge(rows_mm, l + 1)
                sc.activation(rowsA, PS[0:8, 0:N], ACT.Copy).then_inc(rows_ready, 1)
                for t in range(l, NT - 1):
                    h_out(l, t, 0)
                    h_out(l, t, 1)
                act.wait_ge(r_T, l + 1)
                for q in range(3):
                    n = (500, 500, 250)[q]
                    sc.activation(rowsR[:, 500 * q:500 * q + n], bank(q, n, 8), ACT.Copy).then_inc(rowsR_ready, 1)
                h_out(l, NT - 1, 0)
                bcol = vcols[:, 32 + 8 * l:40 + 8 * l]

                def side(n, kind, half, h, base=SIDE):
                    act.wait_ge(side_mm, n + 1)
                    settle(act)
                    if kind < 2:
                        ins = sc.activation(rbc[half][kind][0:P, :], PS[0:P, base:base + HALF], ACT.Copy)
                    else:
                        src_ = PS[:, base:base + 640].rearrange("p (t n) -> p t n", t=5)[:, :, 0:P]
                        k = 2 * h + kind - 2
                        dst_ = featT[:, ds(k, 1), HALF * half:HALF * half + HALF].rearrange("p a (t n) -> p (a t) n", t=5)
                        ins = sc.activation(dst_, src_, ACT.Relu, bias=bcol[:, ds(k, 1)])
                    ins.then_inc(side_out, 1)

                s0 = SIDES * l

                def sums_out(b, u, first):
                    if not first:
                        act.wait_ge(side_mm, s0 + 4 * u)
                    for it in (1, 3):
                        act.wait_ge(sums, b * 5 - 4 + it)
                        sc.activation(osum[0:P, it, :], bank(it, HX, P), ACT.Copy).then_inc(o_act, 1)

                def half_body(h, half, first, second=False):
                    u = 2 * h + half
                    b = 2 * HEADS * l + u
                    act.wait_ge(side_out, s0 + (2 if first else 4 if second else 4 * u - 2))
                    for j in range(NT + 1):
                        if j < NT:
                            if j < RING - 1 and not (first and l == 0):
                                act.wait_ge(p_used, (b - 1) * (NT - 1) + j + NT - RING + 1)
                            elif j == RING - 1 and not (first and l == 0):
                                act.wait_ge(sums, b * 5)
                            elif j >= RING:
                                act.wait_ge(p_used, b * (NT - 1) + j - RING + 1)
                            settle(act)
                            sc.activation(pring[0:P, j % RING, :], rbc[half][1][0:P, :], ACT.Identity,
                                          bias=as02[0:P, j, ds(h, 1)]).then_inc(low_ready, 1)
                        if j >= 1:
                            act.wait_ge(top_ready, b * NT + j)
                            sc.activation(pring[0:P, (j - 1) % RING, :], pring[0:P, (j - 1) % RING, :],
                                          ACT.Exp).then_inc(exp_ready, 1)
                        if j == 2 and not first:
                            sums_out(b, u, second)
                        if j in (5, 7):
                            side(s0 + 4 * u + (j - 5) // 2 + (2 if first else 0), (j - 5) // 2, 1 - half, h)
                        if j == 9 and l == 0 and not first:
                            act.wait_ge(watt_used, 2 * KD + 4 * u + 4)
                            settle(act)
                        if j in (9, 10) and not first:
                            side(s0 + 4 * u + j - 7, j - 7, 1 - half, h - 1 + half)
                if l == 0:
                    act.wait_ge(watt_used, 2 * KD)
                side(s0, 0, 0, 0, 1536)
                side(s0 + 1, 1, 0, 0, 512)
                h_out(l, NT - 1, 1)
                half_body(0, 0, True)
                half_body(0, 1, False, True)
                with act.Fori(1, HEADS) as h:
                    half_body(h, 0, False)
                    half_body(h, 1, False)
                sums_out(2 * HEADS * (l + 1), 2 * HEADS, False)
                if l == 0:
                    h_out(1, 0, 0)
                side(s0 + 8 * HEADS, 2, 1, HEADS - 1)
                side(s0 + 8 * HEADS + 1, 3, 1, HEADS - 1, 1536)
            for l in range(2):
                layer(l)

            for t in range(NT):
                act.wait_ge(var2, t + 1)
                sc.activation(sd[0:P, t:t + 1], sd[0:P, t:t + 1], ACT.Sqrt).then_inc(std2, 1)
                if t >= 1:
                    tokens_T_out = t - 1
                    act.wait_ge(xn2_T, t)
                    sc.activation(xn2T[:, (t - 1) % 2, :, :],
                                  bank(2 + (t - 1) % 2, KD * P).rearrange("p (k n) -> p k n", k=KD),
                                  ACT.Copy).then_inc(xn2T_ready, 1)
            act.wait_ge(xn2_T, NT)
            sc.activation(xn2T[:, (NT - 1) % 2, :, :],
                          bank(2 + (NT - 1) % 2, KD * P).rearrange("p (k n) -> p k n", k=KD),
                          ACT.Copy).then_inc(xn2T_ready, 1)
            act.wait_ge(lg_sub, 1)
            sc.activation(prob[0:P, :, :], prob[0:P, :, :], ACT.Exp).then_inc(lg_exp, 1)
            act.wait_ge(rt_T, 1)
            for q in range(3):
                n = (500, 500, 250)[q]
                sc.activation(wmT[0:PARTS, 500 * q:500 * q + n], bank(q, n, PARTS), ACT.Copy).then_inc(rt_rows, 1)
            for k in range(2):
                act.wait_ge(rt_T, 2 + k)
                for q in range(3):
                    n = (500, 500, 250)[q]
                    sc.activation(ohT[0:PARTS, k, 500 * q:500 * q + n], bank(3 * (1 - k) + q, n, PARTS),
                                  ACT.Copy).then_inc(rt_rows, 1)

            def expert(e, par):
                for q in range(2):
                    act.wait_ge(xg_T, 2 * e + q + 1)
                    sc.activation(xgT[:, par, 2 * q:2 * q + 2, :],
                                  bank(q, 2 * CAPP).rearrange("p (k n) -> p k n", k=2), ACT.Copy).then_inc(xgT_ready, 1)
                for m in range(FM):
                    act.wait_ge(up_mm, e * FM + m + 1)
                    settle(act)
                    sc.activation(hT[:, m, :], bank(2 + m % 2, CAPP), ACT.Gelu,
                                  bias=b1cols[:, ds(e * FM + m, 1)]).then_inc(up_ready, 1)
            with act.Fori(0, NE // 2) as q:
                for par in range(2):
                    expert(q * 2 + par, par)

        @block.vector
        def _(dve):
            v = nc.vector
            st = Steps(dve, dve_step)
            dve.wait_ge(l_x, 16)
            for t in range(NT):
                ins = v.bn_stats(out=stat[0:P, t, :], in_=xs[0:P, t, :])
            st.link(ins)
            for t in range(NT):
                ins = v.bn_aggr(out=mv[0:P, t, :], in_=stat[0:P, t, :])
            st.link(ins)
            v.tensor_scalar(sd[0:P, :], mv[0:P, :, 1], EPS_LN, None, ALU.add).then_inc(var_eps, 1)
            dve.wait_ge(l_grp, 16)
            st.link(v.tensor_copy(grpF[0:NG, :], grpI[0:NG, :]))
            dve.wait_ge(l_edge, 32)
            v.tensor_copy(edgeF[0:CR, :, :], edgeI[0:CR, :, :]).then_inc(edge_f, 1)
            v.tensor_reduce(out=gmm[0:NG, 0:1], in_=grpF[0:NG, :], axis=AX.X, op=ALU.min)
            st.link(v.tensor_reduce(out=gmm[0:NG, 1:2], in_=grpF[0:NG, :], axis=AX.X, op=ALU.max))
            dve.wait_ge(pool_const, CONST["gdn"])
            v.tensor_scalar(gdiag[0:NG, 0, :], identF[0:NG, 0:NG], gmm[0:NG, 0:1], None, ALU.mult)
            v.tensor_scalar(gdiag[0:NG, 1, :], identF[0:NG, 0:NG], gmm[0:NG, 1:2], None, ALU.mult).then_inc(g_cols, 1)
            dve.wait_ge(std, 1)
            st.link(v.reciprocal(rstd[0:P, :], sd[0:P, :]))
            for t in range(NT):
                v.tensor_scalar(xs[0:P, t, :], xs[0:P, t, :], mv[0:P, t, 0:1], rstd[0:P, t:t + 1],
                                ALU.subtract, ALU.mult).then_inc(xn_ready, 1)
            dve.wait_ge(edge_T, 1)
            v.tensor_copy(edgeT[0:CE, :], bank(0, 2 * NCH, CE)).then_inc(edge_cols, 1)
            dve.wait_ge(g_bc, 1)
            v.tensor_scalar(hit[0:NT, :], bank(1, NG, NT), thi[0:NT, :], None, ALU.is_le)
            st.link(v.tensor_scalar(hit2[0:NT, :], bank(1, NG, NT, NG), tlo[0:NT, :], None, ALU.is_ge))
            st.link(v.tensor_tensor(out=hit[0:NT, :], in0=hit[0:NT, :], in1=hit2[0:NT, :], op=ALU.mult))
            v.tensor_tensor(out=hitv[0:NT, 0, :], in0=hit[0:NT, :], in1=gup[0:NT, :], op=ALU.mult)
            st.link(v.tensor_tensor(out=hitv[0:NT, 1, :], in0=hit[0:NT, :], in1=gdn[0:NT, :], op=ALU.mult))
            v.tensor_reduce(out=bnd[0:NT, 1:2], in_=hitv[0:NT, 0, :], axis=AX.X, op=ALU.max)
            st.link(v.tensor_reduce(out=bnd[0:NT, 0:1], in_=hitv[0:NT, 1, :], axis=AX.X, op=ALU.max))
            v.tensor_scalar(bnd[0:NT, 0:1], bnd[0:NT, 0:1], -1.0, float(NG), ALU.mult, ALU.add)
            st.link(v.tensor_scalar(bnd[0:NT, 1:2], bnd[0:NT, 1:2], 1.0, None, ALU.max))
            st.link(v.tensor_scalar(bnd[0:NT, 3:4], bnd[0:NT, 1:2], -1.0, None, ALU.add))
            st.link(v.tensor_tensor(out=bnd[0:NT, 0:1], in0=bnd[0:NT, 0:1], in1=bnd[0:NT, 3:4], op=ALU.min))
            v.tensor_tensor(out=bnd[0:NT, 3:4], in0=bnd[0:NT, 0:1], in1=bnd[0:NT, 1:2], op=ALU.subtract)
            v.tensor_tensor(out=bnd[0:NT, 2:3], in0=bnd[0:NT, 1:2], in1=bnd[0:NT, 0:1],
                            op=ALU.subtract).then_inc(g_rows, 1)
            dve.wait_ge(g_rows, 2)
            v.tensor_copy(bndI[0:1, 0:2 * NT], bank(1, 2 * NT, 1, 128))
            v.tensor_scalar(bndI[0:1, 2 * NT:3 * NT], bank(1, NT, 1, 128 + 2 * NT), float(NG * NT), None,
                            ALU.add).then_inc(g_ready, 1)
            dve.wait_ge(v_T, 3)
            v.tensor_copy(b1cols[:, :], bank(2, 128)).then_inc(v_cols, 1)
            v.tensor_copy(vcols[:, :], bank(2, 48, 128, 128)).then_inc(v_cols, 1)
            v.tensor_copy(gwT[:, :, :], bank(2, KD * NE, 128, 256).rearrange("p (k e) -> p k e", k=KD)).then_inc(v_cols, 1)

            dve.wait_ge(pool_const, CONST["iotaN"])
            dve.wait_ge(g_ready, 1)

            def onehots(t):
                lo = dve.value_load(bndI[0:1, ds(t, 1)], min_val=0, max_val=NG * NT)
                hi = dve.value_load(bndI[0:1, ds(t + NT, 1)], min_val=1, max_val=NG * NT)
                shift = dve.value_load(bndI[0:1, ds(t + 2 * NT, 1)], min_val=0, max_val=NG * NT + NG)
                with dve.Fori(lo, hi) as r:
                    g = nc.s_assert_within(r + shift - NG * NT, 0, NG - 1)
                    for k in range(GC):
                        n = r * GC + k
                        dve.wait_ge(oh_free, n + 1)
                        v.tensor_scalar(ohD[0:CE, k, 0:P], iotaN[0:CE, ds(t * P, P)],
                                        edgeT[0:CE, ds(g * GC + (NCH + k), 1)], None, ALU.is_equal)
                        v.tensor_scalar(ohS[0:CE, k, :], iotaN[0:CE, :],
                                        edgeT[0:CE, ds(g * GC + k, 1)], None, ALU.is_equal).then_inc(oh_ready, 1)

            def make_mask(t, par):
                dve.wait_ge(ctmp_ready, t + 1)
                v.tensor_scalar(mask[0:P, ds(t, 1), :].rearrange("p a n -> p (a n)"), ctmp[0:P, par, :], 0.0, MASKED,
                                ALU.is_equal, ALU.mult).then_inc(mask_ready, 1)
            def att2_sums(k, q):
                i, c = q // 2, q % 2
                dve.wait_ge(watt_ready, 2 * KD + 4 * k + q + 1)
                v.tensor_reduce(out=wa[1][:, ds(k, 1), 4 * i + 2 * c:4 * i + 2 * c + 2],
                                in_=prod.rearrange("p (h c) -> p h c", h=2).unsqueeze(1), axis=AX.X,
                                op=ALU.add).then_inc(watt_used, 1)

            def att_sums(l, k):
                for i in range(2):
                    dve.wait_ge(watt_ready, 2 * k + i + 1 + 2 * KD * l)
                    v.tensor_reduce(out=wa[l][:, ds(k, 1), 4 * i:4 * i + 4],
                                    in_=watt[:, i, :].rearrange("p (h c) -> p h c", h=HEADS).unsqueeze(1),
                                    axis=AX.X, op=ALU.add).then_inc(watt_used, 1)
            onehots(0)
            onehots(1)
            make_mask(0, 0)
            with dve.Fori(1, NT // 2) as q:
                for par in range(2):
                    onehots(q * 2 + par)
                    make_mask(q * 2 + par - 1, 1 - par)
                att_sums(0, q - 1)
            make_mask(NT - 1, 1)

            def layer(l):
                nonlocal_n0 = l * 2 * HEADS * NT
                dve.wait_ge(cols_T, l + 1)
                st.link(v.tensor_copy(asd[0:P, :, :], bank(6, 8 * NT, P).rearrange("p (t r) -> p t r", t=NT)))
                cols_ready_ = v.tensor_scalar(as02[0:P, :, :], asd[0:P, :, 0:4], SLOPE, None, ALU.mult)
                cols_ready_.then_inc(cols_ready, 1)
                for h in range(HEADS):
                    dve.wait_ge(mbc, HEADS * l + h + 1)
                    for t in range(NT):
                        n = (HEADS * l + h) * NT + t
                        if n >= 2:
                            dve.wait_ge(m_tile, n - 1)
                        ins = v.tensor_tensor_reduce(out=junkb[0:P, t % 2, :], in0=mask[0:P, t, :],
                                                     in1=PS[0:P, 1536 * (h % 2):1536 * (h % 2) + N],
                                                     scale=1.0, scalar=MASKED * 10, op0=ALU.add, op1=ALU.max,
                                                     accum_out=mx[0:P, t, h:h + 1])
                        ins.then_inc(m_tile, 1)
                dve.wait_ge(m_tile, HEADS * NT * (l + 1))
                ad = asd[0:P, :, 4:8]
                st.link(v.tensor_tensor(out=mx[0:P, :, :], in0=mx[0:P, :, :], in1=ad, op=ALU.add))
                st.link(v.tensor_scalar(mlk[0:P, :, :], mx[0:P, :, :], SLOPE, None, ALU.mult))
                st.link(v.tensor_tensor(out=mx[0:P, :, :], in0=mx[0:P, :, :], in1=mlk[0:P, :, :], op=ALU.max))
                v.tensor_scalar(mlk[0:P, :, :], ad, SLOPE, None, ALU.mult)
                st.link(v.tensor_tensor(out=rr[0:P, :, 0:4], in0=ad, in1=mx[0:P, :, :], op=ALU.subtract))
                v.tensor_tensor(out=rr[0:P, :, 4:8], in0=mlk[0:P, :, :], in1=mx[0:P, :, :],
                                op=ALU.subtract).then_inc(r_cols, 1)
                s0 = SIDES * l

                def weights(b, j, half):
                    dve.wait_ge(exp_ready, b * NT + j + 1)
                    p = pring[0:P, j % RING, :]
                    v.tensor_tensor(out=p, in0=p, in1=CT[0:P, j, HALF * half:HALF * half + HALF],
                                    op=ALU.mult).then_inc(p_ready, 1)

                def sums_out(b, u, first):
                    if not first:
                        dve.wait_ge(side_mm, s0 + 4 * u)
                    for it in (0, 2, 4):
                        dve.wait_ge(sums, b * 5 - 4 + it)
                        v.tensor_copy(osum[0:P, it, :], bank(it, HX, P)).then_inc(o_dve, 1)

                def divide(b):
                    dve.wait_ge(o_dve, 3 * b)
                    dve.wait_ge(o_act, 2 * b)
                    v.tensor_scalar(rsum[0:P, 0, :], osum[0:P, :, HID], EPS_SM, None, ALU.add).then_inc(s_eps, 1)
                    dve.wait_ge(s_eps, b)
                    v.reciprocal(rsum[0:P, 1, :], rsum[0:P, 0, :]).then_inc(s_inv, 1)
                    dve.wait_ge(s_inv, b)
                    v.tensor_tensor(out=osum[0:P, :, 0:HID], in0=osum[0:P, :, 0:HID],
                                    in1=rsum[0:P, 1, :].unsqueeze(2).to_broadcast([P, 5, HID]), op=ALU.mult).then_inc(o_norm, 1)

                def half_body(h, half, first, second=False):
                    u = 2 * h + half
                    b = 2 * HEADS * l + u
                    dve.wait_ge(side_out, s0 + (2 if first else 4 if second else 4 * u - 2))
                    for j in range(NT + 1):
                        if j < NT:
                            dve.wait_ge(low_ready, b * NT + j + 1)
                            p = pring[0:P, j % RING, :]
                            v.scalar_tensor_tensor(out=p, in0=rbc[half][0][0:P, :], scalar=asd[0:P, j, ds(h, 1)], in1=p,
                                                   op0=ALU.add, op1=ALU.max).then_inc(top_ready, 1)
                        if j >= 1:
                            weights(b, j - 1, half)
                        if j == 2 and not first:
                            sums_out(b, u, second)
                        if j == 4 and not first:
                            divide(b)
                        if l == 0 and 5 <= j < 9:
                            att2_sums(u, j - 5)
                half_body(0, 0, True)
                half_body(0, 1, False, True)
                with dve.Fori(1, HEADS) as h:
                    half_body(h, 0, False)
                    half_body(h, 1, False)
                sums_out(2 * HEADS * (l + 1), 2 * HEADS, False)
                divide(2 * HEADS * (l + 1))
            assert NT // 2 - 1 == KD
            for l in range(2):
                layer(l)

            for t in range(NT):
                dve.wait_ge(fc_mm, t + 1)
                dve.wait_ge(xr_used, t + 1)
                st.link(v.tensor_tensor(out=x2[0:P, t, :], in0=bank(FCB[t % 3], D, P), in1=x2[0:P, t, :], op=ALU.add))
                st.link(v.bn_stats(out=stat[0:P, t, :], in_=x2[0:P, t, :]))
                st.link(v.bn_aggr(out=mv[0:P, t, :], in_=stat[0:P, t, :]))
                v.tensor_scalar(sd[0:P, t:t + 1], mv[0:P, t, 1:2], EPS_LN, None, ALU.add).then_inc(var2, 1)
                dve.wait_ge(std2, t + 1)
                st.link(v.reciprocal(rstd[0:P, t:t + 1], sd[0:P, t:t + 1]))
                v.tensor_scalar(xn2[0:P, t, 0:D], x2[0:P, t, :], mv[0:P, t, 0:1], rstd[0:P, t:t + 1],
                                ALU.subtract, ALU.mult).then_inc(xn2_ready, 1)
            dve.wait_ge(lg_mm, NT)
            dve.wait_ge(l_gb, 16)
            pr = prob[0:P, :, :]

            def over_tiles(col):
                return col.unsqueeze(1).to_broadcast([P, NT, NE])

            def over_experts(col):
                return col.unsqueeze(2).to_broadcast([P, NT, NE])
            st.link(v.tensor_tensor(out=pr, in0=bank(4, NT * NE, P).rearrange("p (t e) -> p t e", t=NT),
                                    in1=over_tiles(gb_bc[0:P, :]), op=ALU.add))
            st.link(v.tensor_reduce(out=red[0:P, :], in_=pr, axis=AX.X, op=ALU.max))
            v.tensor_tensor(out=pr, in0=pr, in1=over_experts(red[0:P, :]), op=ALU.subtract).then_inc(lg_sub, 1)
            dve.wait_ge(lg_exp, 1)
            st.link(v.tensor_reduce(out=red[0:P, :], in_=pr, axis=AX.X, op=ALU.add))
            st.link(v.reciprocal(red2[0:P, :], red[0:P, :]))
            st.link(v.tensor_tensor(out=pr, in0=pr, in1=over_experts(red2[0:P, :]), op=ALU.mult))
            pe_ = pr.unsqueeze(3).to_broadcast([P, NT, NE, NE])
            pf = pr.unsqueeze(2).to_broadcast([P, NT, NE, NE])
            low_ = lowE[0:P, :, :].unsqueeze(1).to_broadcast([P, NT, NE, NE])
            c1v, c2v = cmp1[0:P], cmp2[0:P]
            dve.wait_ge(pool_const, CONST["lowP"])
            v.tensor_tensor(out=c1v, in0=pf, in1=pe_, op=ALU.is_gt)
            st.link(v.tensor_tensor(out=c2v, in0=pf, in1=pe_, op=ALU.is_equal))
            st.link(v.tensor_tensor(out=c2v, in0=c2v, in1=low_, op=ALU.mult))
            st.link(v.tensor_tensor(out=c1v, in0=c1v, in1=c2v, op=ALU.add))
            rk = rank8[0:P, :, :]
            st.link(v.tensor_reduce(out=rk, in_=c1v, axis=AX.X, op=ALU.add))
            for k in range(2):
                ins = v.tensor_scalar(oh2[0:P, k, :, :, :], rk.unsqueeze(2).to_broadcast([P, NT, 3, NE]), float(k), None,
                                      ALU.is_equal)
            st.link(ins)
            st.link(v.tensor_scalar(rk, rk, float(TOPK), None, ALU.is_lt))
            w_, pt = wm[0:P, :, :], part[0:P, :, :]
            st.link(v.tensor_tensor(out=w_, in0=pr, in1=rk, op=ALU.mult))
            st.link(v.tensor_scalar(rk, rk, -1.0, None, ALU.add))
            st.link(v.tensor_tensor(out=w_, in0=w_, in1=rk, op=ALU.add))
            st.link(v.tensor_scalar(w_, w_, BIG, None, ALU.mult))
            for k in range(2):
                st.link(v.tensor_copy(pt, w_))
                v.tensor_copy(wm3[0:P, :, k, :], pt)
                st.link(v.tensor_tensor(out=w_, in0=w_, in1=pt, op=ALU.subtract))
            v.tensor_copy(wm3[0:P, :, 2, :], w_).then_inc(routed, 1)
            for k in range(2):
                tmp = cmp1[0:P, :, 0, :] if k == 0 else cmp1[0:P, :, 1, :]
                tmp2 = cmp2[0:P, :, 0, :] if k == 0 else cmp2[0:P, :, 1, :]
                v.tensor_tensor(out=tmp, in0=oh2[0:P, k, :, 0, :], in1=pr, op=ALU.mult)
                st.link(v.tensor_tensor(out=tmp2, in0=oh2[0:P, k, :, 0, :], in1=over_tiles(eiota[0:P, :]), op=ALU.mult))
                v.tensor_reduce(out=g2[0:P, k, :], in_=tmp, axis=AX.X, op=ALU.add)
                st.link(v.tensor_reduce(out=e2[0:P, k, :], in_=tmp2, axis=AX.X, op=ALU.add))
            v.tensor_scalar(g2big[0:P, :, :], g2[0:P, :, :], BIG, None, ALU.mult)
            dve.wait_ge(pool_const, CONST["number"])
            v.tensor_copy(xn2[0:P, :, D + 1], g2[0:P, 0, :])
            v.tensor_copy(xn2[0:P, :, D + 2], g2[0:P, 1, :])
            v.tensor_copy(xn2[0:P, :, D + 3], e2[0:P, 0, :])

            def slots(t0, t1):
                dve.wait_ge(cnt_used, 2 * t1)
                c = [cnt[0:P, a_, :, t0:t1] for a_ in range(3)]
                kp, ee = keep[0:P, :, t0:t1], e2[0:P, :, t0:t1]
                st.link(v.tensor_tensor(out=c[0], in0=c[0], in1=c[1], op=ALU.add))
                st.link(v.tensor_tensor(out=c[0], in0=c[0], in1=c[2], op=ALU.add))
                v.tensor_scalar(kp, c[0], float(CAP), None, ALU.is_lt)
                st.link(v.tensor_scalar(ee, ee, float(CAPP), float(-NO_SLOT), ALU.mult, ALU.add))
                st.link(v.tensor_tensor(out=c[0], in0=c[0], in1=ee, op=ALU.add))
                st.link(v.tensor_tensor(out=c[0], in0=c[0], in1=kp, op=ALU.mult))
                v.tensor_scalar(slotI[0:P, :, t0:t1], c[0], float(NO_SLOT), None, ALU.add).then_inc(slots_ready, 1)
            st.link(v.memset(cnt[0:P, :, :, :], 0.0))
            for i in range(2 * NT):
                t, k = i // 2, i % 2
                if i >= 2:
                    dve.wait_ge(cnt_used, i - 1)
                dve.wait_ge(cnt_mm, i + 1)
                row = PS[0:P, 1536 * (i % 2):1536 * (i % 2) + N]
                own = g2big[0:P, k, t:t + 1]
                if t:
                    v.tensor_scalar(junk[0:P, i % 2, 0:P * t], row[:, 0:P * t], own, None, ALU.is_ge, ALU.add,
                                    accum_out=cnt[0:P, 0, k, t:t + 1])
                v.tensor_scalar(junk[0:P, i % 2, P * t:N], row[:, P * t:N], own, None, ALU.is_gt, ALU.add,
                                accum_out=cnt[0:P, 1, k, t:t + 1])
                v.scalar_tensor_tensor(out=junk2[0:P, i % 2, :], in0=row[:, P * t:P * t + P], scalar=own, in1=lowP[0:P, :],
                                       op0=ALU.is_equal, op1=ALU.mult,
                                       accum_out=cnt[0:P, 2, k, t:t + 1]).then_inc(cnt_used, 1)
                if (t + 1) in [t1 for _, t1 in BATCHES] and k == 1:
                    slots(*BATCHES[[t1 for _, t1 in BATCHES].index(t + 1)])

            def expert(e, par, q, first):
                dve.wait_ge(xr_in[par], q * 16 + 16)
                last = xr[0:TS, par, :, :]
                v.tensor_scalar(idxI[0:TS, par, :], last[:, :, D], -1.0, float(N), ALU.mult, ALU.add).then_inc(idx_ready, 1)
                v.tensor_scalar(gate[0:TS, 2, :], last[:, :, D + 3], eiota[0:TS, ds(e, 1)], None,
                                ALU.is_equal).then_inc(meta_step, 1)
                dve.wait_ge(meta_step, 3 * e + 1)
                v.tensor_scalar(gate[0:TS, 3, :], gate[0:TS, 2, :], 0.0, None, ALU.is_equal)
                v.tensor_tensor(out=gate[0:TS, 2, :], in0=gate[0:TS, 2, :], in1=last[:, :, D + 1], op=ALU.mult).then_inc(meta_step, 1)
                dve.wait_ge(meta_step, 3 * e + 2)
                v.tensor_tensor(out=gate[0:TS, 3, :], in0=gate[0:TS, 3, :], in1=last[:, :, D + 2], op=ALU.mult).then_inc(meta_step, 1)
                dve.wait_ge(meta_step, 3 * e + 3)
                v.tensor_tensor(out=gate[0:TS, par, :], in0=gate[0:TS, 2, :], in1=gate[0:TS, 3, :],
                                op=ALU.add).then_inc(gate_ready, 1)
                for d in range(KD):
                    dve.wait_ge(dn_mm, e * KD + d + 1)
                    if not (first and par == 0 and d < 2):
                        dve.wait_ge(y_T, e * KD + d - 1)
                    v.tensor_scalar(yT[:, d % 2, :], bank(4 + d % 2, CAPP), vcols[:, ds(e * KD + d, 1)], None,
                                    ALU.add).then_inc(y_ready, 1)
                    if d == 1:
                        dve.wait_ge(gate_ready, e + 1)
                        dve.wait_ge(er_in[par], q * 32 + 32)
                    if d >= 1:
                        rows_out(e, par, d - 1)
                rows_out(e, par, KD - 1)

            def rows_out(e, par, d):
                dve.wait_ge(y_T, e * KD + d + 1)
                for t in range(2):
                    o = er[0:TS, par, t, 128 * d:128 * d + 128]
                    ins = v.scalar_tensor_tensor(out=o, in0=bank(6 + d % 2, 128, TS, 128 * t), scalar=gate[0:TS, par, t:t + 1],
                                                 in1=o, op0=ALU.mult, op1=ALU.add)
                ins.then_inc(er_ready, 1)
            expert(0, 0, 0, True)
            expert(1, 1, 0, True)
            with dve.Fori(1, NE // 2) as q:
                for par in range(2):
                    expert(q * 2 + par, par, q, False)
        @block.tensor
        def _(pe):
            te = nc.tensor
            pe.sem_inc(oh_free, GC)
            pe.sem_inc(sel_used, 1)
            pe.wait_ge(pool_const, CONST["ones"])

            def transpose(o, i_, n, k=None):
                return te.transpose(o, i_, identF[0:n, 0:n])
            pe.wait_ge(edge_f, 1)
            for i in range(4):
                ins = transpose(bank(0, CR, CE, CR * i), edgeF[0:CR, i, :], CR)
            ins.then_inc(edge_T, 1)
            pe.wait_ge(g_cols, 1)
            te.matmul(bank(1, 2 * NG, NT), ones[0:NG, 0:NT], gdiag[0:NG, :, :].rearrange("p a g -> p (a g)"),
                      start=True, stop=True).then_inc(g_bc, 1)
            pe.wait_ge(l_v1, 16)
            transpose(bank(2, 128), vrow, 128).then_inc(v_T, 1)
            pe.wait_ge(l_v2, 48)
            transpose(bank(2, 48, 128, 128), vrow2[0:48, :], 48).then_inc(v_T, 1)
            pe.wait_ge(l_v3, 16)
            for k in range(KD):
                ins = transpose(bank(2, NE, 128, 256 + NE * k), vrow3[0:NE, 128 * k:128 * k + 128], NE)
            ins.then_inc(v_T, 1)
            pe.wait_ge(pool_const, CONST["tri10"])
            pe.wait_ge(g_rows, 1)
            eye = identF[0:NT, 0:NT]
            te.matmul(bank(1, NT, 1, 128), bnd[0:NT, 2:3], tri10[0:NT, 0:NT], start=True, stop=True)
            te.matmul(bank(1, NT, 1, 128 + NT), bnd[0:NT, 2:3], tri10[0:NT, 0:NT], start=True, stop=False)
            te.matmul(bank(1, NT, 1, 128 + NT), bnd[0:NT, 2:3], eye, start=False, stop=True)
            te.matmul(bank(1, NT, 1, 128 + 2 * NT), bnd[0:NT, 0:1], eye, start=True, stop=False)
            te.matmul(bank(1, NT, 1, 128 + 2 * NT), bnd[0:NT, 3:4], tri10[0:NT, 0:NT], start=False,
                      stop=True).then_inc(g_rows, 1)
            for t in range(NT):
                pe.wait_ge(xn_ready, t + 1)
                if t >= 2:
                    pe.wait_ge(xnT_ready, t - 1)
                for k in range(KD):
                    ins = transpose(bank(6 + t % 2, P, 128, P * k), xs[0:P, t, 128 * k:128 * k + 128], P)
                ins.then_inc(xn_T, 1)

            pe.wait_ge(pool_const, CONST["wideI"])
            pe.wait_ge(g_ready, 1)
            pe.wait_ge(edge_cols, 1)
            pe.wait_ge(v_cols, 3)
            COLS = ((0, 512), (512, 1024), (1024, N))

            def counts(t, par, first):
                if not first:
                    pe.wait_ge(ctmp_ready, t - 1)
                lo = pe.value_load(bndI[0:1, ds(t, 1)], min_val=0, max_val=NG * NT)
                hi = pe.value_load(bndI[0:1, ds(t + NT, 1)], min_val=1, max_val=NG * NT)
                for c, (a0, a1) in enumerate(COLS):
                    te.matmul(bank(3 * par + c, a1 - a0, P), identB[0:P, 0:P],
                              wideI[0:P, ds(N - P - t * P + a0, a1 - a0)], start=True, stop=False)
                with pe.Fori(lo, hi) as r:
                    for k in range(GC):
                        n = r * GC + k
                        pe.wait_ge(oh_ready, n + 1)
                        for c, (a0, a1) in enumerate(COLS):
                            ins = te.matmul(bank(3 * par + c, a1 - a0, P), ohD[0:CE, k, 0:P], ohS[0:CE, k, a0:a1],
                                            start=False, stop=False)
                        ins.then_inc(oh_free, 1)
                for c in range(3):
                    ins = te.matmul(bank(3 * par + c, 1, P), wideI[0:P, 0:P], wideI[0:P, 0:1], start=False, stop=True)
                ins.then_inc(c_done, 1)

            def counts_T(t, par, first=False):
                pe.wait_ge(ctmp_ready, t + 1)
                for q in range(3):
                    if q == 2:
                        pe.wait_ge(ct_ready, 3 * t + 1)
                    elif q == 0 and not first:
                        pe.wait_ge(ct_ready, 3 * t)
                    for b in range((4, 4, 2)[q]):
                        j = 4 * q + b
                        ins = transpose(bank(6 + q % 2, P, P, P * b), ctmp[0:P, par, P * j:P * j + P], P)
                    ins.then_inc(c_T, 1)
            pe.wait_ge(xnT_ready, NT)
            counts(0, 0, True)
            counts(1, 1, True)
            counts_T(0, 0, True)
            with pe.Fori(1, NT // 2) as q:
                for par in range(2):
                    counts(q * 2 + par, par, False)
                    counts_T(q * 2 + par - 1, 1 - par)
            counts_T(NT - 1, 1)

            def layer(l):
                K = (KD, KC)[l]
                F = (xnT, featT)[l]
                Wl = (W1s, W2s)[l]
                if l == 0:
                    pe.wait_ge(watt_used, 2 * KD)
                    pe.wait_ge(ct_ready, 3 * NT)
                    pe.wait_ge(l_W1, 16)
                else:
                    pe.wait_ge(side_out, SIDES)

                def h_part(l_, t, c):
                    n = 2 * NT * l_ + 2 * t + c
                    if n >= 2:
                        pe.wait_ge(h_ready, n - 1)
                    Kh, Fh, Wh = (KD, KC)[l_], (xnT, featT)[l_], (W1s, W2s)[l_]
                    for k in range(Kh):
                        ins = te.matmul(bank(7 - c, 512, P), Fh[:, k, P * t:P * t + P], Wh[:, k, 512 * c:512 * c + 512],
                                        start=k == 0, stop=k == Kh - 1)
                    ins.then_inc(h_mm, 1)
                pe.wait_ge(pool_const, CONST["sel"])
                for c, (a0, a1) in enumerate(COLS):
                    for k in range(K):
                        ins = te.matmul(bank(c, a1 - a0, 8), wa[l][:, k, :], F[:, k, a0:a1], start=k == 0, stop=k == K - 1)
                ins.then_inc(rows_mm, 1)
                pe.wait_ge(rows_ready, l + 1)
                if l:
                    pe.wait_ge(h_ready, 2 * NT + 2)
                for t in range(NT):
                    ins = te.transpose(bank(6, 8, P, 8 * t), rowsA[:, P * t:P * t + P], identF[0:8, 0:8])
                ins.then_inc(cols_T, 1)

                def spread(h):
                    if h >= 2:
                        pe.wait_ge(m_tile, (HEADS * l + h - 1) * NT)
                    for c, (a0, a1) in enumerate(COLS):
                        ins = te.matmul(bank(3 * (h % 2) + c, a1 - a0, P), sel[:, h, :], rowsA[:, a0:a1], start=True, stop=True)
                    ins.then_inc(mbc, 1)
                spread(0)
                spread(1)
                pe.wait_ge(cols_ready, l + 1)
                for t in range(l, NT - 1):
                    h_part(l, t, 0)
                    h_part(l, t, 1)
                    if t == 2:
                        spread(2)
                    if t == (5, 4)[l]:
                        spread(3)
                pe.wait_ge(r_cols, l + 1)
                for t in range(NT):
                    ins = transpose(bank(t // 4, P, 8, P * (t % 4)), rr[0:P, t, :], P)
                ins.then_inc(r_T, 1)
                h_part(l, NT - 1, 0)
                pe.wait_ge(rowsR_ready, 3 * (l + 1))
                s0 = SIDES * l

                def side(n, kind, half, first=False, base=SIDE):
                    if not first:
                        pe.wait_ge(side_out, n)
                    if kind < 2:
                        for a0, a1 in ((0, 512), (512, HALF)):
                            ins = te.matmul(PS[0:P, base + a0:base + a1], selcur[:, kind, :],
                                            rowsR[:, HALF * half + a0:HALF * half + a1], start=True, stop=True)
                        ins.then_inc(side_mm, 1)
                    else:
                        for it in range(5):
                            ins = transpose(PS[:, base + 128 * it:base + 128 * it + P],
                                            osum[0:P, it, 128 * (kind - 2):128 * (kind - 1)], P)
                        ins.then_inc(side_mm, 1)

                def heads_sel(h):
                    pe.wait_ge(sel_cur, 2 * (h + 1) + 2 * (HEADS + 1) * l)

                def half_body(h, half, first, second=False):
                    u = 2 * h + half
                    b = 2 * HEADS * l + u
                    for j in range(NT):
                        pe.wait_ge(p_ready, b * NT + j + 1)
                        for it in range(5):
                            if j == 0 and not (first and l == 0):
                                if it % 2:
                                    pe.wait_ge(o_act, 2 * b - 1 + it // 2)
                                else:
                                    pe.wait_ge(o_dve, 3 * b - 2 + it // 2)
                            ins = te.matmul(bank(it, HX, P), pring[0:P, j % RING, P * it:P * it + P],
                                            hx[0:P, j, ds(h, 1), :].rearrange("p a c -> p (a c)"),
                                            start=j == 0, stop=j == NT - 1)
                            if j == NT - 1:
                                ins.then_inc(sums, 1)
                        if j < NT - 1:
                            ins.then_inc(p_used, 1)
                        if j in (1, 3):
                            n = s0 + 4 * u + j // 2 + (2 if first else 0)
                            if half == 1 and j == 1:
                                heads_sel(h + 1)
                            side(n, j // 2, 1 - half)
                            if half == 0 and j == 3:
                                pe.wait_ge(side_mm, n + 1)
                                pe.sem_inc(sel_used, 1)
                        if j in (5, 7) and not first:
                            if j == 5:
                                pe.wait_ge(o_norm, b)
                            side(s0 + 4 * u + j // 2, j // 2, 1 - half)
                heads_sel(0)
                side(s0, 0, 0, True, 1536)
                side(s0 + 1, 1, 0, True, 512)
                h_part(l, NT - 1, 1)
                pe.wait_ge(side_out, s0 + 2)
                pe.wait_ge(h_ready, 2 * NT * (l + 1))
                half_body(0, 0, True)
                half_body(0, 1, False, True)
                with pe.Fori(1, HEADS) as h:
                    half_body(h, 0, False)
                    half_body(h, 1, False)
                pe.wait_ge(side_mm, s0 + 8 * HEADS)
                pe.sem_inc(sel_used, 1)
                pe.wait_ge(side_out, s0 + 8 * HEADS)
                if l == 0:
                    pe.wait_ge(watt_used, 2 * KD + 4 * KC)
                    pe.wait_ge(l_W2, 16)
                    h_part(1, 0, 0)
                else:
                    pe.wait_ge(l_fcW, 16)
                    fc(0)
                pe.wait_ge(o_norm, 2 * HEADS * (l + 1))
                side(s0 + 8 * HEADS, 2, 1)
                pe.wait_ge(o_dve, 3 * 2 * HEADS * (l + 1))
                side(s0 + 8 * HEADS + 1, 3, 1, True, 1536)
                if l == 0:
                    pe.wait_ge(side_out, s0 + 8 * HEADS + 1)
                    h_part(1, 0, 1)
                else:
                    fc(1)

            def fc(t):
                if t >= 3:
                    pe.wait_ge(var2, t - 2)
                for k in range(KC):
                    ins = te.matmul(bank(FCB[t % 3], D, P), featT[:, k, P * t:P * t + P], fcWs[:, k, :], start=k == 0, stop=k == KC - 1)
                ins.then_inc(fc_mm, 1)
            for l in range(2):
                layer(l)

            pe.wait_ge(side_out, 2 * SIDES)

            def tokens_T(t):
                pe.wait_ge(xn2_ready, t + 1)
                if t >= 2:
                    pe.wait_ge(xn2T_ready, t - 1)
                for k in range(KD):
                    ins = transpose(bank(2 + t % 2, P, 128, P * k), xn2[0:P, t, 128 * k:128 * k + 128], P)
                ins.then_inc(xn2_T, 1)

            def logits(t):
                pe.wait_ge(xn2T_ready, t + 1)
                for k in range(KD):
                    ins = te.matmul(bank(4, NE, P, NE * t), xn2T[:, t % 2, k, :], gwT[:, k, :], start=k == 0, stop=k == KD - 1)
                ins.then_inc(lg_mm, 1)
            for t in range(NT):
                if t >= 2:
                    fc(t)
                if t >= 2:
                    logits(t - 2)
                if t >= 1:
                    tokens_T(t - 1)
            tokens_T(NT - 1)
            logits(NT - 2)
            logits(NT - 1)
            pe.wait_ge(routed, 1)
            for k in range(3):
                src_ = wm3[0:P] if k == 0 else oh2[0:P, k - 1]
                if k == 2:
                    pe.wait_ge(rt_rows, 3)
                for t in range(NT):
                    ins = transpose(bank(3 * (k % 2) + t // 4, P, PARTS, P * (t % 4)),
                                    src_[:, t, :, :].rearrange("p a e -> p (a e)"), P)
                ins.then_inc(rt_T, 1)
            pe.wait_ge(rt_rows, 9)
            for i in range(2 * NT):
                t, k = i // 2, i % 2
                if i >= 2:
                    pe.wait_ge(cnt_used, i - 1)
                for c, (a0, a1) in enumerate(COLS):
                    ins = te.matmul(bank(3 * (i % 2) + c, a1 - a0, P), ohT[0:PARTS, k, P * t:P * t + P], wmT[0:PARTS, a0:a1],
                                    start=True, stop=True)
                ins.then_inc(cnt_mm, 1)
            pe.wait_ge(cnt_used, 2 * NT)

            def expert(e, par, q, first):
                pe.wait_ge(xr_in[par], q * 16 + 16)
                for b in range(2):
                    if not (first and par == 0):
                        pe.wait_ge(xgT_ready, 2 * e - 1 + b)
                    for k in (2 * b, 2 * b + 1):
                        for t in range(2):
                            ins = transpose(bank(b, TS, 128, CAPP * (k % 2) + TS * t), xr[0:TS, par, t, 128 * k:128 * k + 128], TS)
                    ins.then_inc(xg_T, 1)
                pe.wait_ge(xgT_ready, 2 * e + 2)
                pe.wait_ge(w1_in[par], q * 16 + 16)
                for m in range(FM):
                    if not (first and par == 0 and m < 2):
                        pe.wait_ge(up_ready, e * FM + m - 1)
                    for k in range(KD):
                        ins = te.matmul(bank(2 + m % 2, CAPP), w1s[par][:, k, 128 * m:128 * m + 128], xgT[:, par, k, :],
                                        start=k == 0, stop=k == KD - 1)
                    ins.then_inc(up_mm, 1)
                pe.wait_ge(w2_in[par], q * 16 + 16)
                for d in range(KD):
                    if not (first and par == 0 and d < 2):
                        pe.wait_ge(y_ready, e * KD + d - 1)
                    for m in range(FM):
                        if d == 0:
                            pe.wait_ge(up_ready, e * FM + m + 1)
                        ins = te.matmul(bank(4 + d % 2, CAPP), w2s[par][:, m, 128 * d:128 * d + 128], hT[:, m, :],
                                        start=m == 0, stop=m == FM - 1)
                    ins.then_inc(dn_mm, 1)
                    if d >= 1:
                        y_rows(e, par, d - 1, first)
                y_rows(e, par, KD - 1, first)

            def y_rows(e, par, d, first):
                pe.wait_ge(y_ready, e * KD + d + 1)
                if not (first and par == 0 and d < 2):
                    pe.wait_ge(er_ready, e * KD + d - 1)
                for t in range(2):
                    ins = te.transpose(bank(6 + d % 2, 128, TS, 128 * t), yT[:, d % 2, TS * t:TS * t + TS], identF[:, :])
                ins.then_inc(y_T, 1)
            expert(0, 0, 0, True)
            expert(1, 1, 0, True)
            with pe.Fori(1, NE // 2) as q:
                for par in range(2):
                    expert(q * 2 + par, par, q, False)


_INS = ["x", "src", "dst", "L0_gnn_W1", "L0_gnn_att_src1", "L0_gnn_att_dst1", "L0_gnn_b1", "L0_gnn_W2",
        "L0_gnn_att_src2", "L0_gnn_att_dst2", "L0_gnn_b2", "L0_gnn_fcW", "L0_gnn_fcb", "L0_ffn_gate_w",
        "L0_ffn_gate_b", "L0_ffn_w1", "L0_ffn_b1", "L0_ffn_w2", "L0_ffn_b2"]


def kernel(**inputs):
    import concourse.bacc as _bacc
    from concourse.bass_utils import run_bass_kernel_spmd as _run

    nc = _bacc.Bacc("TRN2", target_bir_lowering=False, num_devices=1)
    arrays, args = {}, []
    for name in _INS:
        a = np.ascontiguousarray(inputs[name])
        arrays["in_" + name] = a
        args.append(nc.dram_tensor("in_" + name, a.shape, mybir.dt.from_np(a.dtype), kind="ExternalInput").ap())
    args.append(nc.dram_tensor("out_x", (N, D), mybir.dt.float32, kind="ExternalOutput").ap())
    program(nc, *args)
    return _run(nc, [arrays], core_ids=[0]).results[0]["out_x"]
```
